# Optimizing a Trainium2 kernel written in Bass

```python
import numpy as np
import jax
import jax.numpy as jnp

def _softmax(x, axis=-1):
    return jax.nn.softmax(x, axis=axis)

def _gelu(x):
    return jax.nn.gelu(x, approximate=True)

def _silu(x):
    return jax.nn.silu(x)

def _sigmoid(x):
    return jax.nn.sigmoid(x)

def _layernorm(x, axis=-1, eps=1e-05):
    m = jnp.mean(x, axis=axis, keepdims=True)
    v = jnp.var(x, axis=axis, keepdims=True)
    return (x - m) / jnp.sqrt(v + eps)

def _scatter_add(tgt, idx, src, axis=0):
    return tgt.at[idx].add(src)

def _segment_sum(src, seg, n):
    return jax.ops.segment_sum(src, seg, n)
kernel_name = 'mk_hybrid_d1_jaxref_r8_65fd55'

def setup_inputs(seed: int=0):
    np.random.seed(seed)
    _w = jnp.asarray

    def _L0_attn_a_setup():
        import jax, jax.numpy as jnp
        import numpy as np
        D_MODEL, HD_DIM, NUM_HEADS = (128, 256, 16)
        HEAD_DIM = HD_DIM // NUM_HEADS
        B, T = (4, 256)
        key = jax.random.key(seed)
        ks = jax.random.split(key, 10)
        s = 0.02
        x = jax.random.normal(ks[0], (B, T, D_MODEL), dtype=jnp.float32)
        conv_w = jax.random.normal(ks[1], (D_MODEL, 1, 4), dtype=jnp.float32) * s
        conv_b = jax.random.normal(ks[2], (D_MODEL,), dtype=jnp.float32) * s
        qk_w = jax.random.normal(ks[3], (HD_DIM, D_MODEL), dtype=jnp.float32) * s
        v_w = jnp.eye(HD_DIM, D_MODEL, dtype=jnp.float32)
        g_w = jax.random.normal(ks[4], (HD_DIM, D_MODEL), dtype=jnp.float32) * s
        g_b = jnp.full((HD_DIM,), 2.0, dtype=jnp.float32)
        o_w = jax.random.normal(ks[5], (D_MODEL, HD_DIM), dtype=jnp.float32) * s
        ln_g = jnp.ones((D_MODEL,), dtype=jnp.float32)
        ln_b = jnp.zeros((D_MODEL,), dtype=jnp.float32)
        idx = jnp.linspace(0.0, 1.0, HEAD_DIM)
        h = jnp.arange(NUM_HEADS, dtype=jnp.float32)[:, None]
        freqs = jnp.where(h > 0, (10.0 ** idx)[None, :] * h, 0.0).astype(jnp.float32)
        gamma = jnp.full((NUM_HEADS, 1, 1), 0.999, dtype=jnp.float32).at[0].set(1.0)
        return {'x': x, 'conv_w': conv_w, 'conv_b': conv_b, 'qk_w': qk_w, 'v_w': v_w, 'g_w': g_w, 'g_b': g_b, 'o_w': o_w, 'ln_g': ln_g, 'ln_b': ln_b, 'freqs': freqs, 'gamma': gamma}
    _L0_attn_a_in = _L0_attn_a_setup()

    def _L0_attn_b_setup():
        import jax, jax.numpy as jnp
        import numpy as np
        B, S, D, H = (2, 256, 128, 16)
        DK = D // H
        THETA = 10000.0

        def _rope_tables(seq_len, d_k, theta):
            pos = jnp.arange(seq_len, dtype=jnp.float32)
            dim = jnp.arange(0, d_k, 2, dtype=jnp.float32)
            inv_freq = 1.0 / theta ** (dim / d_k)
            angle = pos[:, None] * inv_freq[None, :]
            angle = jnp.repeat(angle, 2, axis=-1)
            return (jnp.cos(angle), jnp.sin(angle))

        def _apply_rope(x, cos, sin):
            x1 = x[..., ::2]
            x2 = x[..., 1::2]
            x_perm = jnp.stack([-x2, x1], axis=-1).reshape(x.shape)
            return x * cos + x_perm * sin
        key = jax.random.key(seed)
        ks = jax.random.split(key, 5)
        std = np.sqrt(2.0 / (D + D)).astype(np.float32)
        return {'x': jax.random.normal(ks[0], (B, S, D), dtype=jnp.float32), 'Wq': jax.random.normal(ks[1], (D, D), dtype=jnp.float32) * std, 'Wk': jax.random.normal(ks[2], (D, D), dtype=jnp.float32) * std, 'Wv': jax.random.normal(ks[3], (D, D), dtype=jnp.float32) * std, 'Wo': jax.random.normal(ks[4], (D, D), dtype=jnp.float32) * std}
    _L0_attn_b_in = _L0_attn_b_setup()

    def _L0_ffn_setup():
        import jax, jax.numpy as jnp
        import numpy as np
        DIM = 128
        DEPTH = 2
        HEADS = 8
        DIM_HEAD = 64
        WINDOW = 64
        INNER = HEADS * DIM_HEAD
        HID = int(DIM * 4 * 2 / 3)
        B, N = (2, 1024)
        QK_SCALE = 8.0

        def shift_token(t):
            t1, t2 = jnp.split(t, 2, axis=-1)
            t2 = jnp.pad(t2, ((0, 0), (1, 0), (0, 0)))[:, :-1]
            return jnp.concatenate([t1, t2], axis=-1)

        def l2norm(t):
            return t / jnp.clip(jnp.linalg.norm(t, axis=-1, keepdims=True), 1e-12)

        def rotate_half(x):
            x1, x2 = jnp.split(x, 2, axis=-1)
            return jnp.concatenate([-x2, x1], axis=-1)

        def rotary_xpos(q, k):
            n = q.shape[-2]
            half_idx = jnp.arange(0, DIM_HEAD, 2, dtype=jnp.float32)
            inv_freq = 1.0 / 10000.0 ** (half_idx / DIM_HEAD)
            t = jnp.arange(n, dtype=jnp.float32)
            freqs = t[:, None] * inv_freq[None, :]
            freqs = jnp.concatenate([freqs, freqs], axis=-1)
            base = (half_idx + 0.4 * DIM_HEAD) / (1.4 * DIM_HEAD)
            power = (t - n // 2) / float(WINDOW // 2)
            scale = base[None, :] ** power[:, None]
            scale = jnp.concatenate([scale, scale], axis=-1)
            cos, sin = (jnp.cos(freqs), jnp.sin(freqs))
            q = q * cos * scale + rotate_half(q) * sin * scale
            k = k * cos / scale + rotate_half(k) * sin / scale
            return (q, k)

        def local_attention(q, k, v):
            b, h, n, d = q.shape
            w = n // WINDOW
            bq = q.reshape(b, h, w, WINDOW, d) * QK_SCALE
            bk = k.reshape(b, h, w, WINDOW, d)
            bv = v.reshape(b, h, w, WINDOW, d)

            def look_around(t):
                p = jnp.pad(t, ((0, 0), (0, 0), (1, 0), (0, 0), (0, 0)))
                return jnp.concatenate([p[:, :, :w], p[:, :, 1:]], axis=3)
            bk, bv = (look_around(bk), look_around(bv))
            bt = jnp.arange(n).reshape(w, WINDOW)
            btp = jnp.pad(bt, ((1, 0), (0, 0)), constant_values=-1)
            btk = jnp.concatenate([btp[:w], btp[1:]], axis=1)
            sim = jnp.einsum('bhwid,bhwjd->bhwij', bq, bk)
            i = bt[:, :, None]
            j = btk[:, None, :]
            mask = (i < j) | (i > j + WINDOW) | (j == -1)
            sim = jnp.where(mask, -jnp.finfo(sim.dtype).max, sim)
            attn = jax.nn.softmax(sim, axis=-1)
            out = jnp.einsum('bhwij,bhwjd->bhwid', attn, bv)
            return out.reshape(b, h, n, d)

        def _layer(x, wqkv, qs, ksc, wo, lg, lb, w1, b1, w2, b2):
            b, n, _ = x.shape
            h = shift_token(x)
            qkv = h @ wqkv
            q, k, v = jnp.split(qkv, 3, axis=-1)
            to_heads = lambda t: t.reshape(b, n, HEADS, DIM_HEAD).transpose(0, 2, 1, 3)
            q, k, v = (to_heads(q), to_heads(k), to_heads(v))
            q = l2norm(q) * qs
            k = l2norm(k) * ksc
            q, k = rotary_xpos(q, k)
            o = local_attention(q, k, v)
            o = o.transpose(0, 2, 1, 3).reshape(b, n, INNER)
            x = x + o @ wo
            h = shift_token(x)
            mu = h.mean(-1, keepdims=True)
            var = h.var(-1, keepdims=True)
            h = (h - mu) / jnp.sqrt(var + 1e-05) * lg + lb
            h = h @ w1 + b1
            a, g = jnp.split(h, 2, axis=-1)
            h = a * jax.nn.gelu(g, approximate=False)
            x = x + h @ w2 + b2
            return x
        key = jax.random.key(seed)
        ks = jax.random.split(key, 6)
        return {'x': jax.random.normal(ks[0], (B, N, DIM), jnp.float32), 'wqkv': jax.random.normal(ks[1], (DEPTH, DIM, 3 * INNER), jnp.float32) * 0.02, 'q_scale': jnp.ones((DEPTH, DIM_HEAD), jnp.float32), 'k_scale': jnp.ones((DEPTH, DIM_HEAD), jnp.float32), 'wo': jax.random.normal(ks[2], (DEPTH, INNER, DIM), jnp.float32) * 0.02, 'ln_g': jnp.ones((DEPTH, DIM), jnp.float32), 'ln_b': jnp.zeros((DEPTH, DIM), jnp.float32), 'w1': jax.random.normal(ks[3], (DEPTH, DIM, 2 * HID), jnp.float32) * 0.02, 'b1': jnp.zeros((DEPTH, 2 * HID), jnp.float32), 'w2': jax.random.normal(ks[4], (DEPTH, HID, DIM), jnp.float32) * 0.02, 'b2': jnp.zeros((DEPTH, DIM), jnp.float32)}
    _L0_ffn_in = _L0_ffn_setup()
    _d = {'L0_attn_a_x': _L0_attn_a_in['x'], 'L0_attn_a_conv_w': _L0_attn_a_in['conv_w'], 'L0_attn_a_conv_b': _L0_attn_a_in['conv_b'], 'L0_attn_a_qk_w': _L0_attn_a_in['qk_w'], 'L0_attn_a_v_w': _L0_attn_a_in['v_w'], 'L0_attn_a_g_w': _L0_attn_a_in['g_w'], 'L0_attn_a_g_b': _L0_attn_a_in['g_b'], 'L0_attn_a_o_w': _L0_attn_a_in['o_w'], 'L0_attn_a_ln_g': _L0_attn_a_in['ln_g'], 'L0_attn_a_ln_b': _L0_attn_a_in['ln_b'], 'L0_attn_a_freqs': _L0_attn_a_in['freqs'], 'L0_attn_a_gamma': _L0_attn_a_in['gamma'], 'L0_attn_b_Wq': _L0_attn_b_in['Wq'], 'L0_attn_b_Wk': _L0_attn_b_in['Wk'], 'L0_attn_b_Wv': _L0_attn_b_in['Wv'], 'L0_attn_b_Wo': _L0_attn_b_in['Wo'], 'L0_ffn_wqkv': _L0_ffn_in['wqkv'], 'L0_ffn_q_scale': _L0_ffn_in['q_scale'], 'L0_ffn_k_scale': _L0_ffn_in['k_scale'], 'L0_ffn_wo': _L0_ffn_in['wo'], 'L0_ffn_ln_g': _L0_ffn_in['ln_g'], 'L0_ffn_ln_b': _L0_ffn_in['ln_b'], 'L0_ffn_w1': _L0_ffn_in['w1'], 'L0_ffn_b1': _L0_ffn_in['b1'], 'L0_ffn_w2': _L0_ffn_in['w2'], 'L0_ffn_b2': _L0_ffn_in['b2']}
    _x0 = _d['L0_attn_a_x']
    _d['L0_attn_a_x'] = jax.random.normal(jax.random.fold_in(jax.random.key(seed), 1), (4, 1024, 128), dtype=_x0.dtype)
    del _x0
    return _d

def reference(L0_attn_a_x, L0_attn_a_conv_w, L0_attn_a_conv_b, L0_attn_a_qk_w, L0_attn_a_v_w, L0_attn_a_g_w, L0_attn_a_g_b, L0_attn_a_o_w, L0_attn_a_ln_g, L0_attn_a_ln_b, L0_attn_a_freqs, L0_attn_a_gamma, L0_attn_b_Wq, L0_attn_b_Wk, L0_attn_b_Wv, L0_attn_b_Wo, L0_ffn_wqkv, L0_ffn_q_scale, L0_ffn_k_scale, L0_ffn_wo, L0_ffn_ln_g, L0_ffn_ln_b, L0_ffn_w1, L0_ffn_b1, L0_ffn_w2, L0_ffn_b2):

    def _L0_attn_a_ref(x, conv_w, conv_b, qk_w, v_w, g_w, g_b, o_w, ln_g, ln_b, freqs, gamma):
        import jax, jax.numpy as jnp
        import numpy as np
        D_MODEL, HD_DIM, NUM_HEADS = (128, 256, 16)
        HEAD_DIM = HD_DIM // NUM_HEADS
        B, T = (4, 256)
        Bsz, Tlen, C = x.shape
        H, D = freqs.shape
        xc = jax.lax.conv_general_dilated(x.transpose(0, 2, 1), conv_w, window_strides=(1,), padding=[(3, 0)], feature_group_count=C, dimension_numbers=('NCH', 'OIH', 'NCH'))
        xc = (xc + conv_b[None, :, None]).transpose(0, 2, 1)
        qk = jnp.einsum('btc,ec->bte', xc, qk_w).reshape(Bsz, Tlen, H, D)
        nrm = jnp.maximum(jnp.sqrt(jnp.sum(qk * qk, axis=-1, keepdims=True)), 1e-12)
        q = qk / nrm
        k = q
        v = jnp.einsum('btc,ec->bte', xc, v_w).reshape(Bsz, Tlen, H, D)
        g = jax.nn.sigmoid(jnp.einsum('btc,ec->bte', xc, g_w) + g_b).reshape(Bsz, Tlen, H, D)
        t = jnp.arange(Tlen, dtype=x.dtype)[None, :, None, None]
        angles = t * freqs[None, None]
        k_sh = jnp.concatenate([jnp.zeros_like(k[:, :1]), k[:, :-1]], axis=1)
        state_r = (v * jnp.cos(angles) + v * k_sh) * g
        decay = jnp.power(gamma.reshape(1, 1, H, 1), t)
        mem_r = jnp.cumsum(state_r * decay, axis=1) / (decay + 1e-06)
        out = (mem_r * q).reshape(Bsz, Tlen, H * D)
        out = jnp.einsum('bte,ce->btc', out, o_w)
        mu = jnp.mean(out, axis=-1, keepdims=True)
        var = jnp.mean((out - mu) ** 2, axis=-1, keepdims=True)
        return (out - mu) / jnp.sqrt(var + 1e-05) * ln_g + ln_b

    def _L0_attn_b_ref(x, Wq, Wk, Wv, Wo):
        import jax, jax.numpy as jnp
        import numpy as np
        B, S, D, H = (2, 256, 128, 16)
        DK = D // H
        THETA = 10000.0

        def _rope_tables(seq_len, d_k, theta):
            pos = jnp.arange(seq_len, dtype=jnp.float32)
            dim = jnp.arange(0, d_k, 2, dtype=jnp.float32)
            inv_freq = 1.0 / theta ** (dim / d_k)
            angle = pos[:, None] * inv_freq[None, :]
            angle = jnp.repeat(angle, 2, axis=-1)
            return (jnp.cos(angle), jnp.sin(angle))

        def _apply_rope(x, cos, sin):
            x1 = x[..., ::2]
            x2 = x[..., 1::2]
            x_perm = jnp.stack([-x2, x1], axis=-1).reshape(x.shape)
            return x * cos + x_perm * sin
        seq_len = x.shape[-2]

        def split_heads(t):
            return t.reshape(*t.shape[:-1], H, DK).swapaxes(-3, -2)
        Q = split_heads(jnp.einsum('bsd,od->bso', x, Wq))
        K = split_heads(jnp.einsum('bsd,od->bso', x, Wk))
        V = split_heads(jnp.einsum('bsd,od->bso', x, Wv))
        cos, sin = _rope_tables(seq_len, DK, THETA)
        Q = _apply_rope(Q, cos, sin)
        K = _apply_rope(K, cos, sin)
        scale = 1.0 / np.sqrt(DK).astype(np.float32)
        logits = jnp.einsum('bhnd,bhmd->bhnm', Q, K) * scale
        causal = jnp.tril(jnp.ones((seq_len, seq_len), dtype=bool))
        logits = jnp.where(causal, logits, -jnp.inf)
        probs = jax.nn.softmax(logits, axis=-1)
        attn = jnp.einsum('bhnm,bhmd->bhnd', probs, V)
        attn = attn.swapaxes(-3, -2).reshape(*x.shape[:-1], D)
        return jnp.einsum('bsd,od->bso', attn, Wo)

    def _L0_ffn_ref(x, wqkv, q_scale, k_scale, wo, ln_g, ln_b, w1, b1, w2, b2):
        import jax, jax.numpy as jnp
        import numpy as np
        DIM = 128
        DEPTH = 2
        HEADS = 8
        DIM_HEAD = 64
        WINDOW = 64
        INNER = HEADS * DIM_HEAD
        HID = int(DIM * 4 * 2 / 3)
        B, N = (2, 1024)
        QK_SCALE = 8.0

        def shift_token(t):
            t1, t2 = jnp.split(t, 2, axis=-1)
            t2 = jnp.pad(t2, ((0, 0), (1, 0), (0, 0)))[:, :-1]
            return jnp.concatenate([t1, t2], axis=-1)

        def l2norm(t):
            return t / jnp.clip(jnp.linalg.norm(t, axis=-1, keepdims=True), 1e-12)

        def rotate_half(x):
            x1, x2 = jnp.split(x, 2, axis=-1)
            return jnp.concatenate([-x2, x1], axis=-1)

        def rotary_xpos(q, k):
            n = q.shape[-2]
            half_idx = jnp.arange(0, DIM_HEAD, 2, dtype=jnp.float32)
            inv_freq = 1.0 / 10000.0 ** (half_idx / DIM_HEAD)
            t = jnp.arange(n, dtype=jnp.float32)
            freqs = t[:, None] * inv_freq[None, :]
            freqs = jnp.concatenate([freqs, freqs], axis=-1)
            base = (half_idx + 0.4 * DIM_HEAD) / (1.4 * DIM_HEAD)
            power = (t - n // 2) / float(WINDOW // 2)
            scale = base[None, :] ** power[:, None]
            scale = jnp.concatenate([scale, scale], axis=-1)
            cos, sin = (jnp.cos(freqs), jnp.sin(freqs))
            q = q * cos * scale + rotate_half(q) * sin * scale
            k = k * cos / scale + rotate_half(k) * sin / scale
            return (q, k)

        def local_attention(q, k, v):
            b, h, n, d = q.shape
            w = n // WINDOW
            bq = q.reshape(b, h, w, WINDOW, d) * QK_SCALE
            bk = k.reshape(b, h, w, WINDOW, d)
            bv = v.reshape(b, h, w, WINDOW, d)

            def look_around(t):
                p = jnp.pad(t, ((0, 0), (0, 0), (1, 0), (0, 0), (0, 0)))
                return jnp.concatenate([p[:, :, :w], p[:, :, 1:]], axis=3)
            bk, bv = (look_around(bk), look_around(bv))
            bt = jnp.arange(n).reshape(w, WINDOW)
            btp = jnp.pad(bt, ((1, 0), (0, 0)), constant_values=-1)
            btk = jnp.concatenate([btp[:w], btp[1:]], axis=1)
            sim = jnp.einsum('bhwid,bhwjd->bhwij', bq, bk)
            i = bt[:, :, None]
            j = btk[:, None, :]
            mask = (i < j) | (i > j + WINDOW) | (j == -1)
            sim = jnp.where(mask, -jnp.finfo(sim.dtype).max, sim)
            attn = jax.nn.softmax(sim, axis=-1)
            out = jnp.einsum('bhwij,bhwjd->bhwid', attn, bv)
            return out.reshape(b, h, n, d)

        def _layer(x, wqkv, qs, ksc, wo, lg, lb, w1, b1, w2, b2):
            b, n, _ = x.shape
            h = shift_token(x)
            qkv = h @ wqkv
            q, k, v = jnp.split(qkv, 3, axis=-1)
            to_heads = lambda t: t.reshape(b, n, HEADS, DIM_HEAD).transpose(0, 2, 1, 3)
            q, k, v = (to_heads(q), to_heads(k), to_heads(v))
            q = l2norm(q) * qs
            k = l2norm(k) * ksc
            q, k = rotary_xpos(q, k)
            o = local_attention(q, k, v)
            o = o.transpose(0, 2, 1, 3).reshape(b, n, INNER)
            x = x + o @ wo
            h = shift_token(x)
            mu = h.mean(-1, keepdims=True)
            var = h.var(-1, keepdims=True)
            h = (h - mu) / jnp.sqrt(var + 1e-05) * lg + lb
            h = h @ w1 + b1
            a, g = jnp.split(h, 2, axis=-1)
            h = a * jax.nn.gelu(g, approximate=False)
            x = x + h @ w2 + b2
            return x
        for l in range(DEPTH):
            x = _layer(x, wqkv[l], q_scale[l], k_scale[l], wo[l], ln_g[l], ln_b[l], w1[l], b1[l], w2[l], b2[l])
        return x
    x = L0_attn_a_x
    x = x + _L0_attn_a_ref(_layernorm(x, axis=-1), L0_attn_a_conv_w, L0_attn_a_conv_b, L0_attn_a_qk_w, L0_attn_a_v_w, L0_attn_a_g_w, L0_attn_a_g_b, L0_attn_a_o_w, L0_attn_a_ln_g, L0_attn_a_ln_b, L0_attn_a_freqs, L0_attn_a_gamma)
    x = x + _L0_ffn_ref(_layernorm(x, axis=-1), L0_ffn_wqkv, L0_ffn_q_scale, L0_ffn_k_scale, L0_ffn_wo, L0_ffn_ln_g, L0_ffn_ln_b, L0_ffn_w1, L0_ffn_b1, L0_ffn_w2, L0_ffn_b2)
    x = x + _L0_attn_b_ref(_layernorm(x, axis=-1), L0_attn_b_Wq, L0_attn_b_Wk, L0_attn_b_Wv, L0_attn_b_Wo)
    x = x + _L0_ffn_ref(_layernorm(x, axis=-1), L0_ffn_wqkv, L0_ffn_q_scale, L0_ffn_k_scale, L0_ffn_wo, L0_ffn_ln_g, L0_ffn_ln_b, L0_ffn_w1, L0_ffn_b1, L0_ffn_w2, L0_ffn_b2)
    return x

_drawn_inputs = setup_inputs


def setup_inputs(seed=0):
    import zlib

    import numpy as np

    out = dict(_drawn_inputs(seed))
    spreads = {'L0_attn_a_g_b': (2.0, 0.2),
     'L0_attn_a_ln_g': (1.0, 0.2),
     'L0_attn_a_ln_b': (0.0, 0.1),
     'L0_ffn_q_scale': (1.0, 0.6),
     'L0_ffn_k_scale': (1.0, 0.6),
     'L0_ffn_ln_g': (1.0, 0.6),
     'L0_ffn_ln_b': (0.0, 0.8),
     'L0_ffn_b1': (0.0, 0.8),
     'L0_ffn_b2': (0.0, 0.1)}
    factors = {'L0_attn_a_g_w': 64.0,
     'L0_ffn_w1': 4.298,
     'L0_ffn_w2': 4.27,
     'L0_attn_b_Wq': 3.308,
     'L0_attn_b_Wk': 3.186}
    for name, (base, spread) in spreads.items():
        noise = np.random.default_rng([zlib.crc32(name.encode()), seed]).standard_normal(out[name].shape)
        drawn = base * np.exp(spread * noise) if base else spread * noise
        out[name] = jnp.asarray(drawn.astype(out[name].dtype))
    for name, factor in factors.items():
        out[name] = (out[name] * factor).astype(out[name].dtype)
    return out
```

```python
import math
from contextlib import ExitStack

import concourse.bass as bass
from concourse import mybir

P = 128
NB, T = 4, 1024
NT = T // P
PAD = 4
EPS = 1e-5
F32 = mybir.dt.float32
BF16 = mybir.dt.bfloat16
ALU = mybir.AluOpType
ACT = mybir.ActivationFunctionType
AX_X = mybir.AxisListType.X

DEPTH = 2
NH, DH = 8, 64
INNER = NH * DH
NPAIR = NH // 2
WIN = 64
WK = P + WIN
HID_DIM = P * 4 * 2 // 3
NHC = 3
HC = -(-HID_DIM // NHC)
QUAD = 4
NQ = NH // QUAD
NSTEP = NB * NQ
LAG = 3
PR = 4


CT = 2
TABLES = CT + 1 + 10 * CT + 2

BH, BD = 16, 8
BG = 4
NG = NB * BH // BG
PARTS = 3
KS9 = PARTS * PARTS * BD

def hidden(j):
    return min(HC, HID_DIM - j * HC)


class Count:

    def __init__(self, sem, per, credit=0):
        self.sem, self.per, self.credit = sem, per, credit

    def at(self, g, k):
        return g * self.per + (self.credit + k)


def allocators(nc, ctx, prefix):
    def sb(name, shape, dt=F32):
        return ctx.enter_context(nc.sbuf_tensor(prefix + name, shape, dt))

    def ps(name, shape, dt=F32):
        return ctx.enter_context(nc.psum_tensor(prefix + name, shape, dt))

    def sem(name):
        return nc.alloc_semaphore(prefix + name)

    return sb, ps, sem


class Norm:

    N = 512

    def __init__(self, sb, sem, keep, chunks, banks, sq=None):
        self.keep, self.chunks, self.banks = keep, chunks, banks
        self.sq = sb("n_sq", [P, 2, self.N]) if sq is None else sq
        self.hc = sb("n_hc", [P, 2, self.N])
        self.rs = sb("n_rs", [P, 2, self.N])
        self.s_centred = sem("n_centred")
        self.s_squared = sem("n_squared")
        self.s_copied = sem("n_copied")
        self.s_var = sem("n_var")
        self.s_ln = sem("n_ln")
        self.s_rstd = sem("n_rstd")
        self.s_out = sem("n_out")

    def tensor(self, pe, source, ready=None):
        for c in range(self.chunks + 1):
            if c < self.chunks:
                if ready:
                    ready(pe, c)
                if c >= 2:
                    pe.wait_ge(self.s_copied, c - 1)
                pe.matmul(self.banks[c % 2][:, :], self.keep["centre"][:, :], source(c),
                          start=True, stop=True).then_inc(self.s_centred, 1)
            if c >= 1:
                v = c - 1
                pe.wait_ge(self.s_squared, v + 1)
                if v >= 2:
                    pe.wait_ge(self.s_ln, v - 1)
                pe.matmul(self.banks[2 + v % 2][:, :], self.keep["mean"][:, :], self.sq[:, v % 2, :],
                          start=True, stop=True).then_inc(self.s_var, 1)

    def scalar(self, act):
        for c in range(self.chunks + 1):
            if c < self.chunks:
                act.wait_ge(self.s_copied, c + 1)
                if c >= 2:
                    act.wait_ge(self.s_var, c - 1)
                act.activation(self.sq[:, c % 2, :], self.hc[:, c % 2, :], ACT.Square)\
                   .then_inc(self.s_squared, 1)
            if c >= 1:
                v = c - 1
                act.wait_ge(self.s_var, v + 1)
                if v >= 2:
                    act.wait_ge(self.s_out, v - 1)
                act.activation(self.rs[:, v % 2, :], self.banks[2 + v % 2][:, :], ACT.Ln,
                               bias=self.keep["eps"][:, :]).then_inc(self.s_ln, 1)
                act.wait_ge(self.s_ln, v + 1)
                act.activation(self.rs[:, v % 2, :], self.rs[:, v % 2, :], ACT.Exp, scale=-0.5)\
                   .then_inc(self.s_rstd, 1)

    def vector(self, dve, store):
        for c in range(self.chunks + 1):
            if c < self.chunks:
                dve.wait_ge(self.s_centred, c + 1)
                if c >= 2:
                    dve.wait_ge(self.s_out, c - 1)
                    dve.wait_ge(self.s_squared, c - 1)
                dve.tensor_copy(self.hc[:, c % 2, :], self.banks[c % 2][:, :]).then_inc(self.s_copied, 1)
            if c >= 1:
                v = c - 1
                dve.wait_ge(self.s_copied, v + 1)
                dve.wait_ge(self.s_rstd, v + 1)
                store(v, self.hc[:, v % 2, :], self.rs[:, v % 2, :]).then_inc(self.s_out, 1)


def ffn_stage(nc, d, keep, stage):
    X, ident = keep["X"], keep["ident"]
    with nc.cleanup_on_exit(), ExitStack() as ctx:
        sb, ps, sem = allocators(nc, ctx, f"ffn{stage}_")

        Y = sb("Y", [P, 2, NB, PAD + T])
        U = sb("U", [P, NB, PAD + T])
        Wqkv = sb("Wqkv", [P, 3, INNER])
        Wo = sb("Wo", [P, NPAIR, P])
        W1 = sb("W1", [P, 2, NHC, HC])
        W2 = sb("W2", [HC, NHC, P])
        B1 = sb("B1", [HC, 2, NHC])
        B2 = sb("B2", [P, 1])
        LG = sb("LG", [P, 1])
        LB = sb("LB", [P, 1])
        QS = sb("QS", [P, 2, DH])
        rope = sb("rope", [P, 2, NT, 2, DH])
        rope0 = sb("rope0", [P, NT, 2, DH])
        masks = sb("masks", [P, NT, P], BF16)
        H1 = sb("H1", [P, NB, P])
        RAW = sb("RAW", [P, 2, 2, NH, DH])
        SQ = sb("SQ", [P, 2, NH, DH])
        SS = sb("SS", [P, 2 * NH])
        SC = sb("SC", [P, 2, 2 * NH])
        RN = sb("RN", [P, 2, 2 * NH])
        mhalf = sb("mhalf", [P, 2 * NH])
        T1 = sb("T1", [P, 2, 2, NH, DH])
        T2 = sb("T2", [P, 2, 2, NH, DH])
        QK = sb("QK", [P, 2, NPAIR, P])
        QT = sb("QT", [P, 2, NPAIR, 2, P])
        KT = sb("KT", [P, NB, NPAIR, WK])
        Vcur = sb("Vcur", [P, NB, INNER])
        Voff = sb("Voff", [P, NB, INNER])
        NM = sb("NM", [P, PR, QUAD])
        DEN = sb("DEN", [P, PR, QUAD])
        RDEN = sb("RDEN", [P, PR, QUAD])
        PB = sb("PB", [P, PR, QUAD, P])
        PT = sb("PT", [P, 2, QUAD, P])
        OT = sb("OT", [P, NPAIR, NB, P])
        H2 = sb("H2", [P, NB, P])
        HN = sb("HN", [P, NB * P])
        AG = sb("AG", [HC, 2, NHC, NB * P])
        proj_ps = [ps(f"proj{i}", [P, 512]) for i in range(2)]
        score_ps = [ps(f"score{i}", [P, 512]) for i in range(2)]
        turn_ps = [ps(f"turn{i}", [P, 512]) for i in range(2)]
        mlp_ps = [ps(f"mlp{i}", [P, 512]) for i in range(2)]
        norm = Norm(sb, sem, keep, NB * T // Norm.N, [proj_ps[0], proj_ps[1], score_ps[0], score_ps[1]],
                    sq=T1[:, 0, :, :, :].rearrange("p c h k -> p c (h k)"))
        SQ2, HC2, RS = norm.rs[:, 1, :], norm.hc[:, 0, :], norm.rs[:, 0, :]

        s_const, s_w, s_zero, s_scaled, s_added = (sem(n) for n in ("const", "w", "zero", "scaled", "added"))
        s_half = sem("half")
        count = lambda name, per, credit=0: Count(sem(name), per, credit)
        h1_low, h1_high = count("h1_low", 1), count("h1_high", 1)
        qk_proj, v_proj = count("qk_proj", 2 * NB), count("v_proj", NB)
        raw = count("raw", 2 * NB)
        sumsq, clamped, rnorm = count("sumsq", NB, 1), count("clamped", NB, 1), count("rnorm", NB, 2)
        roped, rope_sum, qk = count("roped", NB, 2), count("rope_sum", NB), count("qk", NB, 1)
        qk_turned = count("qk_turned", 2 * NB, 1)
        qt, kshift, kt = count("qt", NB, 1), count("kshift", NB), count("kt", NB, NB)
        vshift, v_ready = count("vshift", NB), count("v_ready", NB, NB)
        scores, negmax, probs = count("scores", NSTEP, NSTEP), count("negmax", NSTEP), count("probs", NSTEP, 2)
        rden, normed = count("rden", NSTEP), count("normed", NSTEP)
        p_turned, pt = count("p_turned", NSTEP, PR), count("pt", NSTEP)
        o, ot = count("o", NSTEP, NSTEP), count("ot", NSTEP, 2)
        MLP_MM = 3 + 2 * NHC + 1
        mlp_mm = count("mlp_mm", MLP_MM, MLP_MM)
        u, h2 = count("u", 1), count("h2", 1)
        centred, squared = count("centred", 1), count("squared", 1)
        lnvar, rstd, hn = count("lnvar", 1), count("rstd", 1), count("hn", 2)
        gate, value = count("gate", NHC, 1), count("value", NHC)
        gelu, hid, ynext = count("gelu", 1), count("hid", 1), count("ynext", 1, NT)

        ORDER = [("mlp", 0), ("proj", 0), ("mlp", 1), ("proj", 1), ("mlp", 2), ("turn", 0), ("quad", 0),
                 ("mlp", 3), ("quad", 1), ("mlp", 4), ("proj", 2), ("turn", 1), ("quad", 2), ("mlp", 5),
                 ("quad", 3), ("proj", 3), ("turn", 2), ("quad", 4), ("quad", 5), ("turn", 3)] + [
                ("quad", s) for s in range(6, NSTEP + LAG)]
        PROJ_USE = [(kind, b) for name, b in ORDER if name in ("proj", "turn")
                    for kind in (("q", "k", "v") if name == "proj" else ("qt", "kt"))]

        def proj_bank(kind, b):
            return proj_ps[PROJ_USE.index((kind, b)) % 2]

        def wait_proj_bank(pe, kind, b, g):
            i = PROJ_USE.index((kind, b)) - 2
            g = g if i >= 0 else g - 1
            was, c = PROJ_USE[i]
            if was in "qk":
                pe.wait_ge(raw.sem, raw.at(g, 2 * c + 1 + "qk".index(was)))
            elif was == "v":
                pe.wait_ge(v_ready.sem, v_ready.at(g, c + 1))
            elif was == "qt":
                pe.wait_ge(qt.sem, qt.at(g, c + 1))
            else:
                pe.wait_ge(kt.sem, kt.at(g, c + 1))

        def groups(eng, enter, attention, mlp):
            def run(g, t, l, with_attention, with_mlp):
                for name, n in ORDER:
                    if name == "mlp":
                        if with_mlp:
                            mlp(n, g - 1, t - 1, l)
                    elif with_attention:
                        attention(name, n, g, t, l)

            with eng.Fori(0, DEPTH) as l:
                enter(l)
                run(l * NT, 0, l, True, False)
                with eng.Fori(1, NT) as t:
                    run(l * NT + t, t, l, True, True)
                run(l * NT + NT, NT, l, False, True)

        def cols(t, late=0):
            return bass.ds(t * P + (PAD - late), P)

        NLOAD = 2 + 5 * NHC + 5 + 2

        block = ctx.enter_context(nc.Block())

        @block.sync
        def _(sp):
            sp.dma_start(masks[:, :, :], d["band"]).then_inc(s_const, 16)
            sp.wait_ge(s_zero, 2)
            with sp.Fori(0, DEPTH) as l:
                sp.wait_ge(ynext.sem, l * NT + NT)

                def load(dst, src):
                    sp.dma_start(dst, src).then_inc(s_w, 16)

                load(Wqkv[:, :, :], d["wqkv"][bass.ds(l, 1), :, :].rearrange("a k (c n) -> k (a c) n", c=3))
                load(Wo[:, :, :], d["wo"][bass.ds(l, 1), :, :].rearrange("a (q k) n -> k (a q) n", k=P))
                for j in range(NHC):
                    n = hidden(j)
                    for h in range(2):
                        at = h * HID_DIM + j * HC
                        load(W1[:, h, j, 0:n], d["w1"][bass.ds(l, 1), :, at:at + n].rearrange("a k n -> k (a n)"))
                        load(B1[0:n, h, j:j + 1], d["b1"][bass.ds(l, 1), at:at + n].rearrange("a n -> n a"))
                    load(W2[0:n, j, :], d["w2"][bass.ds(l, 1), j * HC:j * HC + n, :].rearrange("a k n -> k (a n)"))
                load(B2[:, :], d["b2"][bass.ds(l, 1), :].rearrange("a n -> n a"))
                load(LG[:, :], d["ln_g"][bass.ds(l, 1), :].rearrange("a n -> n a"))
                load(LB[:, :], d["ln_b"][bass.ds(l, 1), :].rearrange("a n -> n a"))
                load(QS[:, 0, :], d["q_scale"][bass.ds(l, 1), :].broadcast_to([P, DH]))
                load(QS[:, 1, :], d["k_scale"][bass.ds(l, 1), :].broadcast_to([P, DH]))
                load(rope0[:, :, :, :], d["rope"][0])
                sp.wait_ge(s_scaled, 3 * l + 1)
                load(rope0[:, :, :, :], d["rope"][1])

        @block.tensor
        def _(pe):
            norm.tensor(pe, lambda c: X[:, c * 512:(c + 1) * 512])
            pe.wait_ge(s_const, 16)
            pe.sem_inc(scores.sem, scores.credit)
            pe.sem_inc(qk_turned.sem, qk_turned.credit)
            pe.sem_inc(p_turned.sem, p_turned.credit)
            pe.sem_inc(o.sem, o.credit)
            pe.sem_inc(mlp_mm.sem, mlp_mm.credit)

            def enter(l):
                pe.wait_ge(s_w, l * (16 * NLOAD) + 16 * NLOAD)

            def attention(name, n, g, t, l):
                if name == "proj":
                    b = n
                    if b == 0:
                        pe.wait_ge(h1_low.sem, h1_low.at(g, 1))
                        pe.wait_ge(h1_high.sem, h1_high.at(g, 1))
                    for c, kind in enumerate("qkv"):
                        wait_proj_bank(pe, kind, b, g)
                        done = v_proj if kind == "v" else qk_proj
                        pe.matmul(proj_bank(kind, b)[:, :], H1[:, b, :], Wqkv[:, c, :], start=True, stop=True)\
                          .then_inc(done.sem, 1)
                if name == "turn":
                    b = n
                    pe.wait_ge(qk.sem, qk.at(g, b + 1))
                    for c, kind in enumerate(("qt", "kt")):
                        wait_proj_bank(pe, kind, b, g)
                        bank = proj_bank(kind, b)
                        for p in range(NPAIR):
                            last = pe.transpose(bank[:, p * P:(p + 1) * P], QK[:, c, p, :], ident[:, :])
                        last.then_inc(qk_turned.sem, 1)
                if name == "quad":
                    s, b, r = n, n // NQ, n % NQ
                    if s < NSTEP:
                        if r == 0:
                            pe.wait_ge(qt.sem, qt.at(g, b + 1))
                            pe.wait_ge(kt.sem, kt.at(g, b + 1))
                        pe.wait_ge(probs.sem, probs.at(g, s - 1))
                        bank = score_ps[s % 2]
                        mask = masks[:, bass.ds(t, 1), :].broadcast_to([P, QUAD, P])
                        pe.matmul(bank[:, :], keep["identb"][:, :], mask, start=True, stop=True)
                        for i in range(QUAD):
                            p, e = (r * QUAD + i) // 2, i % 2
                            for w in range(2):
                                rows = slice(w * WIN, (w + 1) * WIN)
                                last = pe.matmul(bank[rows, i * P:(i + 1) * P], QT[:, b % 2, p, e, rows],
                                                 KT[:, b, p, w * WIN:w * WIN + P], start=False,
                                                 stop=True, skip_group_check=True)
                        last.then_inc(scores.sem, 1)
                    s = n - (LAG - 1)
                    if 0 <= s < NSTEP:
                        pe.wait_ge(normed.sem, normed.at(g, s + 1))
                        pe.wait_ge(ot.sem, ot.at(g, s - 1))
                        for i in range(QUAD):
                            last = pe.transpose(turn_ps[s % 2][:, i * P:(i + 1) * P], PB[:, s % PR, i, :], ident[:, :])
                        last.then_inc(p_turned.sem, 1)
                    s = n - LAG
                    if 0 <= s < NSTEP:
                        b, r = s // NQ, s % NQ
                        pe.wait_ge(pt.sem, pt.at(g, s + 1))
                        if r == 0:
                            pe.wait_ge(v_ready.sem, v_ready.at(g, b + 1))
                        for i in range(QUAD):
                            head, e = r * QUAD + i, i % 2
                            for w, V in enumerate((Voff, Vcur)):
                                at = (i // 2) * P + w * WIN
                                last = pe.matmul(turn_ps[s % 2][e * DH:(e + 1) * DH, at:at + WIN],
                                                 V[:, b, head * DH:(head + 1) * DH],
                                                 PT[:, s % 2, i, w * WIN:(w + 1) * WIN], start=True, stop=True)
                        last.then_inc(o.sem, 1)

            def mlp(n, g, t, l):
                bank = mlp_ps
                if n == 0:
                    pe.wait_ge(ot.sem, ot.at(g, NSTEP))
                    pe.wait_ge(gate.sem, gate.at(g - 1, NHC))
                    for p in range(NPAIR):
                        last = pe.matmul(bank[0][:, :], Wo[:, p, :], OT[:, p, :, :], start=(p == 0),
                                         stop=(p == NPAIR - 1))
                    last.then_inc(mlp_mm.sem, 1)
                if n == 1:
                    pe.wait_ge(h2.sem, h2.at(g, 1))
                    pe.wait_ge(ynext.sem, ynext.at(g - 1, 1))
                    pe.matmul(bank[1][:, :], keep["centre"][:, :], H2[:, :, :], start=True, stop=True)\
                      .then_inc(mlp_mm.sem, 1)
                if n == 2:
                    pe.wait_ge(squared.sem, squared.at(g, 1))
                    pe.wait_ge(u.sem, u.at(g, 1))
                    pe.matmul(bank[0][:, :], keep["mean"][:, :], SQ2, start=True, stop=True)\
                      .then_inc(mlp_mm.sem, 1)
                if n in (3, 4):
                    for j in ((0,) if n == 3 else range(1, NHC)):
                        if j == 0:
                            pe.wait_ge(hn.sem, hn.at(g, 2))
                            pe.wait_ge(centred.sem, centred.at(g, 1))
                            pe.wait_ge(lnvar.sem, lnvar.at(g, 1))
                        else:
                            pe.wait_ge(value.sem, value.at(g, j))
                        pe.matmul(bank[1][0:HC, :], W1[:, 0, j, :], HN[:, :], start=True, stop=True)\
                          .then_inc(mlp_mm.sem, 1)
                        if j:
                            pe.wait_ge(gate.sem, gate.at(g, j))
                        pe.matmul(bank[0][0:HC, :], W1[:, 1, j, :], HN[:, :], start=True, stop=True)\
                          .then_inc(mlp_mm.sem, 1)
                if n == 5:
                    pe.wait_ge(hid.sem, hid.at(g, 1))
                    pe.wait_ge(value.sem, value.at(g, NHC))
                    for j in range(NHC):
                        last = pe.matmul(bank[1][:, :], W2[:, j, :], AG[:, 0, j, :], start=(j == 0),
                                         stop=(j == NHC - 1))
                    last.then_inc(mlp_mm.sem, 1)

            groups(pe, enter, attention, mlp)

        @block.scalar
        def _(act):
            norm.scalar(act)
            act.sem_inc(qt.sem, qt.credit)
            act.sem_inc(v_ready.sem, v_ready.credit)
            act.sem_inc(probs.sem, probs.credit)
            act.sem_inc(ot.sem, ot.credit)
            act.wait_ge(norm.s_out, norm.chunks)
            act.wait_ge(s_zero, 5)

            def enter(l):
                act.wait_ge(s_w, l * (16 * NLOAD) + 16 * NLOAD)

            def attention(name, n, g, t, l):
                if name == "proj":
                    b = n
                    if b == 0:
                        act.wait_ge(ynext.sem, ynext.at(g - NT, 1))
                        act.wait_ge(v_proj.sem, v_proj.at(g, 0)) if not isinstance(g, int) else None
                        act.activation(H1[64:P, :, :], Y[64:P, bass.ds(l, 1), :, cols(t, 1)]
                                       .rearrange("p a b c -> p (a b) c"), ACT.Copy).then_inc(h1_high.sem, 1)
                    act.wait_ge(sumsq.sem, sumsq.at(g, b))
                    act.wait_ge(roped.sem, roped.at(g, b - 1))
                    for c in range(2):
                        act.wait_ge(qk_proj.sem, qk_proj.at(g, 2 * b + c + 1))
                        bank = proj_bank("qk"[c], b)[:, :].rearrange("p (h e) -> p h e", e=DH)
                        act.activation(SQ[:, c, :, :], bank, ACT.Square)
                        act.activation(RAW[:, b % 2, c, :, :], bank, ACT.Copy).then_inc(raw.sem, 1)
                    act.wait_ge(v_proj.sem, v_proj.at(g, b + 1))
                    act.wait_ge(vshift.sem, vshift.at(g, b + 1))
                    bank = proj_bank("v", b)
                    act.activation(Vcur[:, b, :], bank[:, :], ACT.Copy)
                    act.activation(Voff[WIN:P, b, :], bank[0:WIN, :], ACT.Copy).then_inc(v_ready.sem, 1)
                if name == "turn":
                    b = n
                    act.wait_ge(qk_turned.sem, qk_turned.at(g, 2 * b + 1))
                    act.wait_ge(scores.sem, scores.at(g, NQ * (b - 1)))
                    bank = proj_bank("qt", b)[:, :].rearrange("p (q c) -> p q c", q=NPAIR)
                    act.activation(QT[0:DH, b % 2, :, 0, :], bank[0:DH], ACT.Copy)
                    act.activation(QT[DH:P, b % 2, :, 1, :], bank[DH:P], ACT.Copy).then_inc(qt.sem, 1)
                if name == "quad":
                    s = n
                    if s < NSTEP:
                        act.wait_ge(negmax.sem, negmax.at(g, s + 1))
                        act.wait_ge(p_turned.sem, p_turned.at(g, s - PR + 1))
                        for i in range(QUAD):
                            last = act.activation(PB[:, s % PR, i, :], score_ps[s % 2][:, i * P:(i + 1) * P],
                                                  ACT.Exp, bias=NM[:, s % PR, i:i + 1],
                                                  accum_out=DEN[:, s % PR, i:i + 1])
                        last.then_inc(probs.sem, 1)
                    s = n - LAG
                    if 0 <= s < NSTEP:
                        act.wait_ge(o.sem, o.at(g, s + 1))
                        if s == 0:
                            act.wait_ge(mlp_mm.sem, mlp_mm.at(g - 1, 1))
                        b, p = s // NQ, (s % NQ) * QUAD // 2
                        act.activation(OT[:, p:p + QUAD // 2, b, :],
                                       turn_ps[s % 2][:, 0:QUAD // 2 * P].rearrange("p (q c) -> p q c", c=P),
                                       ACT.Copy).then_inc(ot.sem, 1)

            def mlp(n, g, t, l):
                if n == 0:
                    act.wait_ge(u.sem, u.at(g, 1))
                    act.activation(H2[0:64, :, :], U[0:64, :, cols(t)], ACT.Copy)
                    act.activation(H2[64:P, :, :], U[64:P, :, cols(t, 1)], ACT.Copy).then_inc(h2.sem, 1)
                if n == 1:
                    act.wait_ge(centred.sem, centred.at(g, 1))
                    act.activation(SQ2, HC2, ACT.Square).then_inc(squared.sem, 1)
                if n == 2:
                    act.wait_ge(mlp_mm.sem, mlp_mm.at(g, 3))
                    act.activation(RS, mlp_ps[0][:, :], ACT.Ln, bias=keep["eps"][:, :]).then_inc(lnvar.sem, 1)
                    act.wait_ge(lnvar.sem, lnvar.at(g, 1))
                    act.activation(RS, RS, ACT.Exp, scale=-0.5).then_inc(rstd.sem, 1)
                if n in (3, 4):
                    for j in ((0,) if n == 3 else range(1, NHC)):
                        act.wait_ge(mlp_mm.sem, mlp_mm.at(g, 4 + 2 * j))
                        act.activation(AG[:, 0, j, :], mlp_ps[1][0:HC, :], ACT.Identity,
                                       bias=B1[:, 0, j:j + 1]).then_inc(value.sem, 1)
                if n == 4:
                    act.wait_ge(gate.sem, gate.at(g, NHC))
                    act.activation(AG[:, 1, :, :], AG[:, 1, :, :], ACT.Gelu).then_inc(gelu.sem, 1)

            groups(act, enter, attention, mlp)

        @block.vector
        def _(dve):
            dve.memset(W1[:, :, :, :], 0.0).then_inc(s_zero, 1)
            dve.memset(W2[:, :, :], 0.0).then_inc(s_zero, 1)
            dve.memset(Y[:, :, :, 0:PAD], 0.0)
            dve.memset(U[:, :, 0:PAD], 0.0).then_inc(s_zero, 1)
            dve.memset(QT[:, :, :, :, :], 0.0)
            dve.memset(KT[:, :, :, :], 0.0).then_inc(s_zero, 1)
            dve.memset(B1[:, :, :], 0.0).then_inc(s_zero, 1)
            dve.memset(Vcur[:, :, :], 0.0)
            dve.memset(Voff[:, :, :], 0.0).then_inc(s_zero, 1)

            def fill(c, hc, rs):
                b, half = c // 2, c % 2
                return dve.tensor_tensor(Y[:, 0, b, PAD + half * 512:PAD + (half + 1) * 512], hc, rs, ALU.mult)

            norm.vector(dve, fill)
            dve.wait_ge(s_zero, 6)
            dve.wait_ge(norm.s_out, norm.chunks)
            for c in (sumsq, clamped, roped, qk, kt, gate, ynext):
                dve.sem_inc(c.sem, c.credit)

            def enter(l):
                dve.wait_ge(s_w, l * (16 * NLOAD) + 16 * (NLOAD - 1))
                spread = lambda a: a.unsqueeze(1).broadcast_to([P, NT] + list(a.shape[1:]))
                dve.tensor_tensor(rope[:, 0, :, :, :], rope0[:, :, :, :], spread(QS[:, :, :]), ALU.mult)\
                   .then_inc(s_scaled, 1)
                dve.wait_ge(s_w, l * (16 * NLOAD) + 16 * NLOAD)
                for h in range(2):
                    a, b = slice(32 * h, 32 * h + 32), slice(32 - 32 * h, 64 - 32 * h)
                    dve.tensor_tensor(rope[:, 1, :, :, a], rope0[:, :, :, a], spread(QS[:, :, b]), ALU.mult)\
                       .then_inc(s_scaled, 1)
                dve.wait_ge(s_scaled, 3 * l + 3)

            def attention(name, n, g, t, l):
                if name == "proj":
                    b = n
                    if b == 0:
                        dve.wait_ge(ynext.sem, ynext.at(g - NT, 1))
                        dve.wait_ge(v_ready.sem, v_ready.at(g - 1, NB))
                        dve.tensor_copy(H1[0:64, :, :], Y[0:64, bass.ds(l, 1), :, cols(t)]
                                        .rearrange("p a b c -> p (a b) c")).then_inc(h1_low.sem, 1)
                    dve.wait_ge(v_ready.sem, v_ready.at(g - 1, b + 1))
                    dve.wait_ge(o.sem, o.at(g - 1, NQ * (b + 1)))
                    dve.tensor_copy(Voff[0:WIN, b, :], Vcur[WIN:P, b, :]).then_inc(vshift.sem, 1)
                    dve.wait_ge(kt.sem, kt.at(g - 1, b + 1))
                    dve.wait_ge(scores.sem, scores.at(g - 1, NQ * (b + 1)))
                    dve.tensor_copy(KT[:, b, :, 0:WIN], KT[:, b, :, P:WK]).then_inc(kshift.sem, 1)
                    dve.wait_ge(raw.sem, raw.at(g, 2 * b + 2))
                    dve.wait_ge(clamped.sem, clamped.at(g, b))
                    dve.reduce_sum(SS[:, :], SQ[:, :, :, :].rearrange("p c h e -> p (c h) e"), AX_X)\
                       .then_inc(sumsq.sem, 1)
                    tab = lambda k: rope[:, k, bass.ds(t, 1), :, :].rearrange("p a c e -> p (a c) e")
                    spread = lambda a: a.unsqueeze(2).broadcast_to([P, 2, NH, a.shape[-1]])
                    dve.wait_ge(qk.sem, qk.at(g, b - 1))
                    dve.tensor_tensor(T1[:, b % 2, :, :, :], RAW[:, b % 2, :, :, :], spread(tab(0)), ALU.mult)
                    dve.wait_ge(sumsq.sem, sumsq.at(g, b + 1))
                    dve.wait_ge(rnorm.sem, rnorm.at(g, b - 1))
                    dve.tensor_scalar(SC[:, b % 2, :], SS[:, :], 1e-24, None, ALU.max).then_inc(clamped.sem, 1)
                    for h in range(2):
                        a, c = slice(32 * h, 32 * h + 32), slice(32 - 32 * h, 64 - 32 * h)
                        last = dve.tensor_tensor(T2[:, b % 2, :, :, a], RAW[:, b % 2, :, :, c],
                                                 spread(tab(1)[:, :, a]), ALU.mult)
                    last.then_inc(roped.sem, 1)
                if name == "turn":
                    b = n
                    dve.wait_ge(rope_sum.sem, rope_sum.at(g, b + 1))
                    dve.wait_ge(rnorm.sem, rnorm.at(g, b + 1))
                    dve.wait_ge(qk_turned.sem, qk_turned.at(g, 2 * b))
                    dve.tensor_tensor(QK[:, :, :, :].rearrange("p c q (e k) -> p (c q e) k", k=DH),
                                      T1[:, b % 2, :, :, :].rearrange("p c h k -> p (c h) k"),
                                      RN[:, b % 2, :].unsqueeze(2).broadcast_to([P, 2 * NH, DH]), ALU.mult)\
                       .then_inc(qk.sem, 1)
                    dve.wait_ge(qk_turned.sem, qk_turned.at(g, 2 * b + 2))
                    dve.wait_ge(kshift.sem, kshift.at(g, b + 1))
                    dve.tensor_copy(KT[:, b, :, WIN:WK], proj_bank("kt", b)[:, :].rearrange("p (q c) -> p q c", q=NPAIR))\
                       .then_inc(kt.sem, 1)
                if name == "quad":
                    s = n
                    if s < NSTEP:
                        dve.wait_ge(scores.sem, scores.at(g, s + 1))
                        dve.tensor_reduce(NM[:, s % PR, :], score_ps[s % 2][:, :].rearrange("p (i k) -> p i k", i=QUAD),
                                          AX_X, ALU.max, negate=True).then_inc(negmax.sem, 1)
                    s = n - 1
                    if 0 <= s < NSTEP:
                        dve.wait_ge(probs.sem, probs.at(g, s + 1))
                        dve.reciprocal(RDEN[:, s % PR, :], DEN[:, s % PR, :]).then_inc(rden.sem, 1)
                    s = n - (LAG - 1)
                    if 0 <= s < NSTEP:
                        dve.wait_ge(p_turned.sem, p_turned.at(g, s + 1))
                        dve.tensor_copy(PT[:, s % 2, :, :].rearrange("p i k -> p (i k)"), turn_ps[s % 2][:, :]).then_inc(pt.sem, 1)

            def mlp(n, g, t, l):
                if n == 0:
                    dve.wait_ge(mlp_mm.sem, mlp_mm.at(g, 1))
                    dve.tensor_tensor(U[:, :, cols(t)], mlp_ps[0][:, :].rearrange("p (b c) -> p b c", b=NB),
                                      Y[:, bass.ds(l, 1), :, cols(t)].rearrange("p a b c -> p (a b) c"), ALU.add)\
                       .then_inc(u.sem, 1)
                if n == 1:
                    dve.wait_ge(mlp_mm.sem, mlp_mm.at(g, 2))
                    dve.tensor_copy(HC2, mlp_ps[1][:, :]).then_inc(centred.sem, 1)
                if n == 2:
                    dve.wait_ge(centred.sem, centred.at(g, 1))
                    dve.wait_ge(rstd.sem, rstd.at(g, 1))
                    dve.tensor_tensor(HN[:, :], HC2, RS, ALU.mult).then_inc(hn.sem, 1)
                    dve.wait_ge(hn.sem, hn.at(g, 1))
                    dve.tensor_scalar(HN[:, :], HN[:, :], LG[:, :], LB[:, :], ALU.mult, ALU.add)\
                       .then_inc(hn.sem, 1)
                if n in (3, 4):
                    for j in ((0,) if n == 3 else range(1, NHC)):
                        dve.wait_ge(mlp_mm.sem, mlp_mm.at(g, 5 + 2 * j))
                        dve.tensor_scalar(AG[:, 1, j, :], mlp_ps[0][0:HC, :], B1[:, 1, j:j + 1], None, ALU.add)\
                           .then_inc(gate.sem, 1)
                if n == 4:
                    dve.wait_ge(gelu.sem, gelu.at(g, 1))
                    dve.wait_ge(value.sem, value.at(g, NHC))
                    dve.tensor_tensor(AG[:, 0, :, :], AG[:, 0, :, :], AG[:, 1, :, :], ALU.mult).then_inc(hid.sem, 1)
                if n == 5:
                    other = l * -1 + 1
                    dve.wait_ge(mlp_mm.sem, mlp_mm.at(g, MLP_MM))
                    dve.scalar_tensor_tensor(
                        out=Y[:, bass.ds(other, 1), :, cols(t)].rearrange("p a b c -> p (a b) c"),
                        in0=mlp_ps[1][:, :].rearrange("p (b c) -> p b c", b=NB), scalar=B2[:, 0:1],
                        in1=U[:, :, cols(t)], op0=ALU.add, op1=ALU.add).then_inc(ynext.sem, 1)

            groups(dve, enter, attention, mlp)
            dve.wait_ge(ynext.sem, ynext.at(DEPTH * NT - 1, 1))
            for b in range(NB):
                dve.tensor_tensor(X[:, b * T:(b + 1) * T], X[:, b * T:(b + 1) * T], Y[:, 0, b, PAD:PAD + T], ALU.add)\
                   .then_inc(s_added, 1)
            dve.wait_ge(s_added, NB)

        @block.gpsimd
        def _(pool):
            pool.memset(mhalf[:, :], -0.5).then_inc(s_half, 1)
            pool.wait_ge(s_half, 1)
            pool.sem_inc(rnorm.sem, rnorm.credit)

            def attention(name, n, g, t, l):
                if name == "proj":
                    b = n
                    pool.wait_ge(clamped.sem, clamped.at(g, b + 1))
                    pool.tensor_tensor(RN[:, b % 2, :], SC[:, b % 2, :], mhalf[:, :], ALU.pow).then_inc(rnorm.sem, 1)
                    pool.wait_ge(roped.sem, roped.at(g, b + 1))
                    pool.tensor_tensor(T1[:, b % 2, :, :, :], T1[:, b % 2, :, :, :], T2[:, b % 2, :, :, :], ALU.add)\
                        .then_inc(rope_sum.sem, 1)
                if name == "quad":
                    s = n - 1
                    if 0 <= s < NSTEP:
                        pool.wait_ge(rden.sem, rden.at(g, s + 1))
                        pool.tensor_tensor(PB[:, s % PR, :, :], PB[:, s % PR, :, :],
                                           RDEN[:, s % PR, :].unsqueeze(2).broadcast_to([P, QUAD, P]), ALU.mult)\
                            .then_inc(normed.sem, 1)

            groups(pool, lambda l: None, attention, lambda *a: None)


def attn_a_stage(nc, d, keep):
    X, ident = keep["X"], keep["ident"]
    with nc.cleanup_on_exit(), ExitStack() as ctx:
        sb, ps, sem = allocators(nc, ctx, "attn_a_")
        XIN = sb("XIN", [P, NB * NT, P])
        XN = sb("XN", [P, NB, PAD + T])
        Wq, Wv, Wg = sb("Wq", [P, CT, P]), sb("Wv", [P, CT, P]), sb("Wg", [P, CT, P])
        Wo = sb("Wo", [P, CT, P])
        heads16 = sb("heads16", [P, P])
        cw, cb = sb("cw", [P, 4]), sb("cb", [P, 1])
        gb, lg, lb = sb("gb", [P, CT]), sb("lg", [P, 1]), sb("lb", [P, 1])
        freqs, gamma = sb("freqs", [P, CT]), sb("gamma", [P, CT])
        pos = sb("pos", [P, T])
        turns = sb("turns", [P, T])
        ang = sb("ang", [P, T])
        cos = sb("cos", [P, CT, T])
        decay = sb("decay", [P, CT, T])
        rdecay = sb("rdecay", [P, CT, T])
        gpow = sb("gpow", [P, 11, CT])
        ones = sb("ones", [P, T])
        shift = sb("shift", [P, 1])
        XC = sb("XC", [P, T])
        SQ = sb("SQ", [P, T])
        RAW = sb("RAW", [P, T])
        RN = sb("RN", [P, T])
        Q = sb("Q", [P, PAD + T])
        A = sb("A", [P, T])
        G = sb("G", [P, T])
        M = sb("M", [P, T])
        OUT = sb("OUT", [P, CT, T])
        bank = [ps(f"bank{i}", [P, 512]) for i in range(8)]
        norm = Norm(sb, sem, keep, NB * T // 512, bank[0:4])
        qk_ps, ss_ps, v_ps, g_ps = (bank[2 * i:2 * i + 2] for i in range(4))

        s_x, s_w, s_xt, s_xe, s_zero, s_tab, s_gp, s_trig, s_sin = (
            sem(n) for n in ("x", "w", "xt", "xe", "zero", "tab", "gp", "trig", "sin"))
        count = lambda name, per, credit=0: Count(sem(name), per, credit)
        qk_mm, ss_mm, v_mm, g_mm = (count(n, 1, 1) for n in ("qk_mm", "ss_mm", "v_mm", "g_mm"))
        squared, copied, clamped, lnq, rnorm, gated = (
            count(n, 1, 1) for n in ("squared", "copied", "clamped", "lnq", "rnorm", "gated"))
        q_ready, kcos, decayed, av, avg, summed, scaled, out_ready = (
            count(n, 1, 1) for n in ("q_ready", "kcos", "decayed", "av", "avg", "summed", "scaled", "out_ready"))
        conv = count("conv", 4)
        o_mm, c_mm, var_mm = (count(n, 1, 1) for n in ("o_mm", "c_mm", "var_mm"))
        o_sb, hc, hsq, hln, hrs, hx = (count(n, 1, 1) for n in ("o_sb", "hc", "hsq", "hln", "hrs", "hx"))
        hx = count("hxs", 3, 3)
        NWA = 14

        block = ctx.enter_context(nc.Block())

        @block.sync
        def _(sp):
            for b in range(NB):
                sp.dma_start(XIN[:, b * NT:(b + 1) * NT, :], d["x"][b].rearrange("(t p) c -> p t c", p=P)).then_inc(s_x, 16)
            for n in ("ident", "centre", "mean", "eps", "identb"):
                sp.dma_start(keep[n][:, :], d[n]).then_inc(s_x, 16)

        @block.gpsimd
        def _(pool):
            for dst, src in ((pos[:, :], d["pos"].broadcast_to([P, T])), (freqs[:, :], d["freqs"]),
                             (gamma[:, :], d["gamma"]), (cw[:, :], d["conv_w"]), (cb[:, :], d["conv_b"]),
                             (Wq[:, :, :], d["qk_wT"].rearrange("k (c n) -> k c n", c=CT)),
                             (heads16[:, :], d["heads16"]),
                             (Wv[:, :, :], d["v_wT"].rearrange("k (c n) -> k c n", c=CT)),
                             (Wg[:, :, :], d["g_wT"].rearrange("k (c n) -> k c n", c=CT)),
                             (Wo[:, :, :], d["o_wT"].rearrange("(c k) n -> k c n", c=CT)),
                             (gb[:, :], d["g_b"]), (lg[:, :], d["ln_g"]), (lb[:, :], d["ln_b"]),
                             (shift[:, :], d["shift"])):
                pool.dma_start(dst, src).then_inc(s_w, 16)
            pool.wait_ge(s_w, 16 * NWA)
            for c in (kcos, decayed):
                pool.sem_inc(c.sem, c.credit)
            pool.wait_ge(s_tab, TABLES)
            pool.wait_ge(s_sin, CT)
            with pool.Fori(0, NB) as b:
                for c in range(CT):
                    n = b * CT + c
                    pool.wait_ge(gated.sem, gated.at(n, 1))
                    pool.tensor_tensor(G[:, :], G[:, :], decay[:, c, :], ALU.mult).then_inc(decayed.sem, 1)
                    pool.wait_ge(q_ready.sem, q_ready.at(n, 1))
                    pool.wait_ge(summed.sem, summed.at(n, 0))
                    pool.tensor_tensor(A[:, :], cos[:, c, :], Q[:, PAD - 1:PAD - 1 + T], ALU.add)\
                        .then_inc(kcos.sem, 1)

        @block.tensor
        def _(pe):
            pe.wait_ge(s_x, 16 * 9)
            for c in range(NB * T // 512):
                if c >= 2:
                    pe.wait_ge(s_xe, c - 1)
                for i in range(4):
                    last = pe.transpose(bank[4 + c % 2][:, i * P:(i + 1) * P], XIN[:, 4 * c + i, :], ident[:, :])
                last.then_inc(s_xt, 1)
            norm.tensor(pe, lambda c: X[:, c * 512:(c + 1) * 512], lambda pe, c: pe.wait_ge(s_xe, c + 1))
            for c in (qk_mm, ss_mm, v_mm, g_mm, o_mm, c_mm, var_mm):
                pe.sem_inc(c.sem, c.credit)
            pe.wait_ge(s_w, 16 * NWA)
            pe.wait_ge(norm.s_out, norm.chunks)

            def product(banks, weights, source):
                for h in range(2):
                    last = pe.matmul(banks[h][:, :], weights, source[:, h * 512:(h + 1) * 512], start=True, stop=True)
                return last

            with pe.Fori(0, NB) as b:
                pe.wait_ge(conv.sem, conv.at(b, 4))
                for c in range(CT):
                    n = b * CT + c
                    if c == 0:
                        pe.wait_ge(hln.sem, hln.at(b, 0))
                        pe.wait_ge(hc.sem, hc.at(b, 0))
                    pe.wait_ge(copied.sem, copied.at(n, 0))
                    product(qk_ps, Wq[:, c, :], XC).then_inc(qk_mm.sem, 1)
                    pe.wait_ge(gated.sem, gated.at(n, 0))
                    product(g_ps, Wg[:, c, :], XC).then_inc(g_mm.sem, 1)
                    pe.wait_ge(av.sem, av.at(n, 0))
                    product(v_ps, Wv[:, c, :], XC).then_inc(v_mm.sem, 1)
                    pe.wait_ge(squared.sem, squared.at(n, 1))
                    pe.wait_ge(clamped.sem, clamped.at(n, 0))
                    product(ss_ps, heads16[:, :], SQ).then_inc(ss_mm.sem, 1)
                pe.wait_ge(out_ready.sem, out_ready.at(b * CT, CT))
                pe.wait_ge(copied.sem, copied.at(b * CT, CT))
                for h in range(2):
                    for c in range(CT):
                        last = pe.matmul(qk_ps[h][:, :], Wo[:, c, :], OUT[:, c, h * 512:(h + 1) * 512],
                                         start=(c == 0), stop=(c == CT - 1))
                last.then_inc(o_mm.sem, 1)
                pe.wait_ge(o_sb.sem, o_sb.at(b, 1))
                pe.wait_ge(clamped.sem, clamped.at(b * CT, CT))
                product(ss_ps, keep["centre"][:, :], RAW).then_inc(c_mm.sem, 1)
                pe.wait_ge(hsq.sem, hsq.at(b, 1))
                product(qk_ps, keep["mean"][:, :], SQ).then_inc(var_mm.sem, 1)

        def both(banks):
            return banks

        @block.scalar
        def _(act):
            for c in range(NB * T // 512):
                act.wait_ge(s_xt, c + 1)
                act.activation(X[:, c * 512:(c + 1) * 512], bank[4 + c % 2][:, :], ACT.Copy).then_inc(s_xe, 1)
            norm.scalar(act)
            for c in range(CT):
                act.wait_ge(s_trig, 6 * c + 6)
                act.activation(cos[:, c, :], cos[:, c, :], ACT.Sin).then_inc(s_sin, 1)
            for c in (squared, copied, lnq, rnorm, gated, o_sb, hsq, hln, hrs):
                act.sem_inc(c.sem, c.credit)
            act.wait_ge(s_w, 16 * NWA)

            def halves(dst, banks, func, **more):
                for h in range(2):
                    last = act.activation(dst[:, h * 512:(h + 1) * 512], banks[h][:, :], func, **more)
                return last

            with act.Fori(0, NB) as b:
                for c in range(CT):
                    n = b * CT + c
                    act.wait_ge(qk_mm.sem, qk_mm.at(n, 1))
                    if c == 0:
                        act.wait_ge(var_mm.sem, var_mm.at(b, 0))
                        act.wait_ge(c_mm.sem, c_mm.at(b, 0))
                    act.wait_ge(ss_mm.sem, ss_mm.at(n, 0))
                    halves(SQ, qk_ps, ACT.Square).then_inc(squared.sem, 1)
                    act.wait_ge(q_ready.sem, q_ready.at(n, 0))
                    halves(RAW, qk_ps, ACT.Copy).then_inc(copied.sem, 1)
                    act.wait_ge(clamped.sem, clamped.at(n, 1))
                    act.activation(RN[:, :], RN[:, :], ACT.Ln, scale=float(2 ** 20)).then_inc(lnq.sem, 1)
                    act.wait_ge(lnq.sem, lnq.at(n, 1))
                    act.activation(RN[:, :], RN[:, :], ACT.Exp, scale=-0.5, bias=shift[:, :]).then_inc(rnorm.sem, 1)
                    act.wait_ge(g_mm.sem, g_mm.at(n, 1))
                    act.wait_ge(avg.sem, avg.at(n, 0))
                    halves(G, g_ps, ACT.Sigmoid, bias=gb[:, c:c + 1]).then_inc(gated.sem, 1)
                act.wait_ge(o_mm.sem, o_mm.at(b, 1))
                act.wait_ge(q_ready.sem, q_ready.at(b * CT, CT))
                halves(RAW, qk_ps, ACT.Copy).then_inc(o_sb.sem, 1)
                act.wait_ge(hc.sem, hc.at(b, 1))
                act.wait_ge(ss_mm.sem, ss_mm.at(b * CT, CT))
                act.activation(SQ[:, :], M[:, :], ACT.Square).then_inc(hsq.sem, 1)
                act.wait_ge(var_mm.sem, var_mm.at(b, 1))
                act.wait_ge(q_ready.sem, q_ready.at(b * CT, CT))
                halves(RN, qk_ps, ACT.Ln, bias=keep["eps"][:, :]).then_inc(hln.sem, 1)
                act.wait_ge(hln.sem, hln.at(b, 1))
                act.activation(RN[:, :], RN[:, :], ACT.Exp, scale=-0.5).then_inc(hrs.sem, 1)

        @block.vector
        def _(dve):
            dve.memset(XN[:, :, 0:PAD], 0.0)
            dve.memset(Q[:, 0:PAD], 0.0)
            dve.memset(ones[:, :], 1.0).then_inc(s_zero, 1)

            def fill(c, hc, rs):
                b, half = c // 2, c % 2
                return dve.tensor_tensor(XN[:, b, PAD + half * 512:PAD + (half + 1) * 512], hc, rs, ALU.mult)

            norm.vector(dve, fill)
            dve.wait_ge(s_w, 16 * NWA)
            TURN1 = 201 / 32
            TURN2 = 507 * 2.0 ** -18
            TURN3 = 2 * math.pi - TURN1 - TURN2
            BIG = 1.5 * 2.0 ** 23
            k = 0
            for c in range(CT):
                ang_c = cos[:, c, :]

                def done(ins):
                    nonlocal k
                    k += 1
                    ins.then_inc(s_trig, 1)
                    dve.wait_ge(s_trig, k)

                dve.tensor_scalar(ang_c, pos[:, :], freqs[:, c:c + 1], None, ALU.mult).then_inc(s_tab, 1)
                dve.wait_ge(s_tab, c + 1)
                done(dve.tensor_scalar(turns[:, :], ang_c, 1 / (2 * math.pi), 0.25, ALU.mult, ALU.add))
                done(dve.tensor_scalar(turns[:, :], turns[:, :], BIG, None, ALU.add))
                done(dve.tensor_scalar(turns[:, :], turns[:, :], -BIG, None, ALU.add))
                dve.scalar_tensor_tensor(out=ang[:, :], in0=turns[:, :], scalar=-TURN1, in1=ang_c,
                                         op0=ALU.mult, op1=ALU.add).then_inc(s_zero, 1)
                dve.wait_ge(s_zero, 2 + 2 * c)
                dve.scalar_tensor_tensor(out=ang[:, :], in0=turns[:, :], scalar=-TURN2, in1=ang[:, :],
                                         op0=ALU.mult, op1=ALU.add).then_inc(s_zero, 1)
                dve.wait_ge(s_zero, 3 + 2 * c)
                done(dve.scalar_tensor_tensor(out=ang[:, :], in0=turns[:, :], scalar=-TURN3, in1=ang[:, :],
                                              op0=ALU.mult, op1=ALU.add))
                done(dve.tensor_scalar(ang[:, :], ang[:, :], math.pi / 2, 3.1415925, ALU.add, ALU.min))
                done(dve.tensor_scalar(ang_c, ang[:, :], -3.1415925, None, ALU.max))
            dve.tensor_copy(gpow[:, 0, :], gamma[:, :]).then_inc(s_gp, 1)
            for i in range(10):
                dve.wait_ge(s_gp, i + 1)
                dve.tensor_tensor(gpow[:, i + 1, :], gpow[:, i, :], gpow[:, i, :], ALU.mult).then_inc(s_gp, 1)
            dve.memset(decay[:, :, 0:1], 1.0).then_inc(s_tab, 1)
            at = CT + 1
            for i in range(10):
                n = 1 << i
                for c in range(CT):
                    dve.wait_ge(s_tab, at - c)
                    dve.tensor_scalar(decay[:, c, n:2 * n], decay[:, c, 0:n], gpow[:, i, c:c + 1], None, ALU.mult)\
                       .then_inc(s_tab, 1)
                    at += 1
            dve.wait_ge(s_tab, at)
            dve.tensor_scalar(rdecay[:, :, :], decay[:, :, :], 1e-6, None, ALU.add).then_inc(s_tab, 1)
            dve.wait_ge(s_tab, at + 1)
            dve.reciprocal(rdecay[:, :, :], rdecay[:, :, :]).then_inc(s_tab, 1)
            dve.wait_ge(s_tab, at + 2)
            assert at + 2 == TABLES
            for c in (clamped, q_ready, av, avg, summed, scaled, out_ready, hc, hx):
                dve.sem_inc(c.sem, c.credit)
            dve.wait_ge(norm.s_out, norm.chunks)

            with dve.Fori(0, NB) as b:
                tap = lambda j: XN[:, bass.ds(b, 1), PAD - 3 + j:PAD - 3 + j + T].rearrange("p a t -> p (a t)")
                dve.wait_ge(g_mm.sem, g_mm.at(b * CT, 0))
                dve.wait_ge(v_mm.sem, v_mm.at(b * CT, 0))
                dve.tensor_scalar(XC[:, :], tap(3), cw[:, 3:4], cb[:, :], ALU.mult, ALU.add).then_inc(conv.sem, 1)
                for j in range(3):
                    dve.wait_ge(conv.sem, conv.at(b, j + 1))
                    dve.scalar_tensor_tensor(out=XC[:, :], in0=tap(j), scalar=cw[:, j:j + 1], in1=XC[:, :],
                                             op0=ALU.mult, op1=ALU.add).then_inc(conv.sem, 1)
                for c in range(CT):
                    n = b * CT + c
                    dve.wait_ge(ss_mm.sem, ss_mm.at(n, 1))
                    for h in range(2):
                        last = dve.tensor_scalar(RN[:, h * 512:(h + 1) * 512], ss_ps[h][:, :], 1e-24, None, ALU.max)
                    last.then_inc(clamped.sem, 1)
                    dve.wait_ge(rnorm.sem, rnorm.at(n, 1))
                    dve.wait_ge(copied.sem, copied.at(n, 1))
                    dve.wait_ge(kcos.sem, kcos.at(n, 0))
                    dve.tensor_tensor(Q[:, PAD:PAD + T], RAW[:, :], RN[:, :], ALU.mult).then_inc(q_ready.sem, 1)
                    dve.wait_ge(kcos.sem, kcos.at(n, 1))
                    dve.wait_ge(v_mm.sem, v_mm.at(n, 1))
                    for h in range(2):
                        a = A[:, h * 512:(h + 1) * 512]
                        last = dve.tensor_tensor(a, v_ps[h][:, :], a, ALU.mult)
                    last.then_inc(av.sem, 1)
                    dve.wait_ge(av.sem, av.at(n, 1))
                    dve.wait_ge(decayed.sem, decayed.at(n, 1))
                    dve.tensor_tensor(A[:, :], A[:, :], G[:, :], ALU.mult).then_inc(avg.sem, 1)
                    dve.wait_ge(avg.sem, avg.at(n, 1))
                    if c == 0:
                        dve.wait_ge(hsq.sem, hsq.at(b, 0))
                    dve.tensor_tensor_scan(M[:, :], ones[:, :], A[:, :], 0.0, ALU.mult, ALU.add)\
                       .then_inc(summed.sem, 1)
                    dve.wait_ge(summed.sem, summed.at(n, 1))
                    dve.tensor_tensor(M[:, :], M[:, :], rdecay[:, c, :], ALU.mult).then_inc(scaled.sem, 1)
                    dve.wait_ge(scaled.sem, scaled.at(n, 1))
                    dve.wait_ge(q_ready.sem, q_ready.at(n, 1))
                    if c == 0:
                        dve.wait_ge(o_mm.sem, o_mm.at(b, 0))
                    dve.tensor_tensor(OUT[:, c, :], M[:, :], Q[:, PAD:PAD + T], ALU.mult).then_inc(out_ready.sem, 1)
                dve.wait_ge(c_mm.sem, c_mm.at(b, 1))
                dve.wait_ge(out_ready.sem, out_ready.at(b * CT, CT))
                for h in range(2):
                    last = dve.tensor_copy(M[:, h * 512:(h + 1) * 512], ss_ps[h][:, :])
                last.then_inc(hc.sem, 1)
                dve.wait_ge(hrs.sem, hrs.at(b, 1))
                dve.wait_ge(hc.sem, hc.at(b, 1))
                dve.tensor_tensor(A[:, :], M[:, :], RN[:, :], ALU.mult).then_inc(hx.sem, 1)
                x = X[:, bass.ds(b * T, T)]
                dve.wait_ge(hx.sem, hx.at(b, 1))
                dve.scalar_tensor_tensor(out=A[:, :], in0=A[:, :], scalar=lg[:, 0:1], in1=x,
                                         op0=ALU.mult, op1=ALU.add).then_inc(hx.sem, 1)
                dve.wait_ge(hx.sem, hx.at(b, 2))
                dve.tensor_scalar(x, A[:, :], lb[:, :], None, ALU.add).then_inc(hx.sem, 1)
            dve.wait_ge(hx.sem, hx.at(NB - 1, 3))


def wait(eng, sem, value):
    if not isinstance(value, int) or value > 0:
        eng.wait_ge(sem, value)


def attn_b_stage(nc, d, keep):
    X = keep["X"]
    with nc.cleanup_on_exit(), ExitStack() as ctx:
        sb, ps, sem = allocators(nc, ctx, "attn_b_")
        XN = sb("XN", [P, NB, T])
        XB = sb("XB", [P, T])
        W = sb("W", [P, 4, P])
        Wv, Wo = sb("Wv", [P, P]), sb("Wo", [P, P])
        rope = sb("rope", [P, 4, T])
        causal = sb("causal", [P, 2, P], BF16)
        T1, T2 = sb("T1", [P, T]), sb("T2", [P, T])
        R = sb("R", [P, T])
        RP = sb("RP", [P, 2, PARTS, T], BF16)
        VB = sb("VB", [P, NG, NT, BG, BD + 1])
        VQ = sb("VQ", [P, BG, NT, BD + 1])
        QS = sb("QS", [KS9 + PARTS, BG, T], BF16)
        KS = sb("KS", [KS9 + PARTS, BG, T], BF16)
        ones = sb("ones", [PARTS, BG, T], BF16)
        NX = sb("NX", [P, 2, 2, NT])
        NM = sb("NM", [P, 2, NT])
        NP = sb("NP", [P, 2, PARTS, NT], BF16)
        NR = sb("NR", [P, 2, NT])
        zeros = sb("zeros", [P, NT])
        MT = sb("MT", [PARTS * NT, 2, P], BF16)
        PT = sb("PT", [P, 4, T])
        OS = sb("OS", [BD + 1, 2, T])
        OA = sb("OA", [P, 2, T])
        DA = sb("DA", [P, 2, T])
        s1_ps = [ps(f"s1_{i}", [P, 512]) for i in range(2)]
        o_ps = [ps(f"o_{i}", [P, 512]) for i in range(2)]
        s2_ps = [ps(f"s2_{i}", [P, 1024]) for i in range(2)]
        qk_dram = nc.dram_tensor("attn_b_qk_parts", (2, PARTS, NB * P, T), BF16, kind="Internal").ap()
        o_dram = nc.dram_tensor("attn_b_o", (NB * BH, BD + 1, T), F32, kind="Internal").ap()
        norm = Norm(sb, sem, keep, NB * T // 512, [o_ps[0], o_ps[1], s1_ps[0], s1_ps[1]])

        s_w, s_set, s_zeros = sem("w"), sem("set"), sem("zeros")
        count = lambda name, per: Count(sem(name), per)
        xb, ab_mm, v_mm = count("xb", 1), count("ab_mm", 4), count("v_mm", 1)
        turned, rsum, p1, r1, p2, p3 = (count("rotated", 4), count("rsum", 2), count("p1", 2), count("r1", 2),
                                        count("p2", 2), count("p3", 2))
        s_parts_out = [sem("q_out"), sem("k_out")]
        v_copied = count("v_copied", 1)
        UNITS = 13
        TURN = 3
        s_load = [sem(f"load{h}") for h in range(BG)]
        s_rows = [sem(f"rows{h}") for h in range(BG)]
        s_stored = [sem(f"stored{i}") for i in range(2)]
        s1_mm, s1_read = count("s1_mm", UNITS * BG), count("s1_read", UNITS * BG)
        parts = count("parts", 4 * BG)
        maxima = count("maxima", BG)
        s2_mm, probs, pv = count("s2_mm", NT * BG), count("probs", NT * BG), count("pv", NT * BG)
        vq, o_read = count("vq", BG), count("o_read", 2 * BG)
        s_back = [sem("back0"), sem("back1")]
        s_rden, s_scaled, s_out_mm, s_added = sem("rden"), sem("scaled"), sem("out_mm"), sem("added")

        CHUNKS = [(i, c) for i in reversed(range(NT)) for c in range(i // 4 + 1)]
        SLOTS = [1, 1, 1, 1, 1, 1, 2, 2, 2, 1]
        assert len(CHUNKS) == UNITS - 1 and sum(SLOTS) == UNITS

        def over_groups(eng, step, last=NG):
            for h in range(BG):
                step(0, h, True, h >= 1, h >= 2)
            with eng.Fori(1, last) as n:
                for h in range(BG):
                    step(n, h, True, True, True)

        def over_sequences(eng, work):
            work(0)
            with eng.Fori(1, NB) as b:
                work(b)

        def chunk_keys(i, c):
            return c * 512, min((c + 1) * 512, (i + 1) * P)

        block = ctx.enter_context(nc.Block())

        @block.sync
        def _(sp):
            for i, n in enumerate(("WqT", "WqpT", "WkT", "WkpT")):
                sp.dma_start(W[:, i, :], d[n]).then_inc(s_w, 16)
            sp.dma_start(Wv[:, :], d["WvT"]).then_inc(s_w, 16)
            sp.dma_start(rope[:, :, :], d["rope"]).then_inc(s_w, 16)
            sp.dma_start(causal[:, :, :], d["causal"]).then_inc(s_w, 16)
            sp.dma_start(Wo[:, :], d["WoT"]).then_inc(s_w, 16)
            sp.wait_ge(s_set, 1)
            sp.dma_start(KS[KS9:KS9 + PARTS, :, :], ones[:, :, :]).then_inc(s_w, 16)

            def store_parts(b):
                for w in range(2):
                    sp.wait_ge(p3.sem, p3.at(b, w + 1))
                    sp.dma_start(qk_dram[w][:, bass.ds(b * P, P), :].rearrange("a c t -> c a t"), RP[:, w, :, :])\
                      .then_inc(s_parts_out[w], 16)

            over_sequences(sp, store_parts)
            for w in range(2):
                sp.wait_ge(s_parts_out[w], 16 * NB)

            def load(n, h):
                rows = bass.ds(n * (BG * BD) + h * BD, BD)
                for a in range(PARTS):
                    at = slice(a * PARTS * BD, (a + 1) * PARTS * BD)
                    q = qk_dram[0][a, rows, :].unsqueeze(0).broadcast_to([PARTS, BD, T])
                    k = qk_dram[1][:, rows, :]
                    sp.dma_start(QS[at, h, :], q).then_inc(s_load[h], 16)
                    sp.dma_start(KS[at, h, :], k).then_inc(s_load[h], 16)

            for h in range(BG):
                load(0, h)

            def step(n, h, s1, turn, s2, ahead=True):
                k = (h - 1) % BG
                if turn:
                    sp.wait_ge(s1_read.sem, s1_read.at(n, UNITS * h + TURN + 1))
                    sp.dma_start(QS[KS9:KS9 + PARTS, k, :], MT[:, k % 2, :]).then_inc(s_rows[k], 16)
                if s2:
                    k = (h - 2) % BG
                    if ahead:
                        sp.wait_ge(s2_mm.sem, s2_mm.at(n, NT * (h - 1)))
                        load(n + (h - 2 - k) // BG + 1, k)
                    sp.wait_ge(o_read.sem, o_read.at(n, 2 * (h - 1)))
                    sp.dma_start(o_dram[bass.ds(n * BG + h - 2, 1), :, :].rearrange("a e t -> (a e) t"),
                                 OS[:, h % 2, :]).then_inc(s_stored[h % 2], 16)

            over_groups(sp, step, NG - 1)
            for h in range(BG):
                step(NG - 1, h, True, True, True, ahead=h < 2)
            step(NG, 0, False, True, True, ahead=False)
            step(NG, 1, False, False, True, ahead=False)
            for i in range(2):
                sp.wait_ge(s_stored[i], 16 * NG * BG // 2)
            for b in range(NB):
                if b >= 2:
                    sp.wait_ge(s_out_mm, b - 1)
                heads = o_dram[b * BH:(b + 1) * BH]
                sp.dma_start(OA[:, b % 2, :], heads[:, 0:BD, :]).then_inc(s_back[b % 2], 16)
                sp.dma_start(DA[:, b % 2, :], heads[:, BD:BD + 1, :].broadcast_to([BH, BD, T]))\
                  .then_inc(s_back[b % 2], 16)

        @block.tensor
        def _(pe):
            norm.tensor(pe, lambda c: X[:, c * 512:(c + 1) * 512])
            pe.wait_ge(s_w, 16 * 9)
            pe.wait_ge(norm.s_out, norm.chunks)

            def project(b):
                pe.wait_ge(xb.sem, xb.at(b, 1))
                for w in range(4):
                    wait(pe, turned.sem, turned.at(b, w - 1))
                    for h in range(2):
                        last = pe.matmul(s2_ps[w % 2][:, h * 512:(h + 1) * 512], W[:, w, :],
                                         XB[:, h * 512:(h + 1) * 512], start=True, stop=True)
                    last.then_inc(ab_mm.sem, 1)
                wait(pe, v_copied.sem, v_copied.at(b, 0))
                for t in range(NT):
                    last = pe.matmul(s1_ps[t // 4][:, t % 4 * P:(t % 4 + 1) * P], XB[:, t * P:(t + 1) * P], Wv[:, :],
                                     start=True, stop=True)
                last.then_inc(v_mm.sem, 1)

            over_sequences(pe, project)
            pe.wait_ge(v_copied.sem, NB)
            pe.wait_ge(turned.sem, 4 * NB)

            def max_unit(n, h, u):
                i, c = CHUNKS[u if u < TURN else u - 1]
                lo, hi = chunk_keys(i, c)
                bank = s1_ps[(UNITS * h + u) % 2]
                wait(pe, s1_read.sem, s1_read.at(n, UNITS * h + u - 1))
                diagonal = hi == (i + 1) * P
                if diagonal:
                    pe.matmul(bank[:, hi - lo - P:hi - lo], keep["identb"][:, :], causal[:, 0, :], start=True,
                              stop=True)
                pe.matmul(bank[:, 0:hi - lo], QS[0:KS9, h, i * P:(i + 1) * P], KS[0:KS9, h, lo:hi],
                          start=not diagonal, stop=True, skip_group_check=True).then_inc(s1_mm.sem, 1)

            def turn_unit(n, h):
                bank = s1_ps[(UNITS * h + TURN) % 2]
                k = (h - 1) % BG
                wait(pe, s1_read.sem, s1_read.at(n, UNITS * h + TURN - 1))
                pe.wait_ge(parts.sem, parts.at(n, 4 * h))
                pe.matmul(bank[0:PARTS * NT, 0:P], NP[:, k % 2, :, :].rearrange("p a i -> p (a i)"),
                          keep["identb"][:, :], start=True, stop=True).then_inc(s1_mm.sem, 1)

            def exp_unit(n, h, j):
                k = (h - 2) % BG
                width = T - j * P
                bank = s2_ps[j % 2]
                wait(pe, probs.sem, probs.at(n, NT * (h - 2) + j - 1))
                if j == 0:
                    pe.wait_ge(s_rows[k], 16 * (n + 1 + (h - 2 - k) // BG))
                pe.matmul(bank[:, 0:P], keep["identb"][:, :], causal[:, 1, :], start=True, stop=True)
                for lo in range(0, width, 512):
                    hi = min(width, lo + 512)
                    last = pe.matmul(bank[:, lo:hi], KS[:, k, j * P:(j + 1) * P], QS[:, k, j * P + lo:j * P + hi],
                                     start=lo > 0, stop=True, skip_group_check=True)
                last.then_inc(s2_mm.sem, 1)

            def value_unit(n, h, j):
                k = (h - 2) % BG
                if j == 0:
                    wait(pe, o_read.sem, o_read.at(n, 2 * (h - 2)))
                    pe.wait_ge(vq.sem, vq.at(n, h - 1))
                pe.wait_ge(probs.sem, probs.at(n, NT * (h - 2) + j + 1))
                for half in range(j // 4, 2):
                    lo, hi = max(j * P, half * 512), (half + 1) * 512
                    last = pe.matmul(o_ps[half][0:BD + 1, lo - half * 512:512], VQ[:, k, j, :],
                                     PT[:, j % 4, lo - j * P:hi - j * P], start=(j == 0), stop=(j % 4 == 3),
                                     skip_group_check=True)
                last.then_inc(pv.sem, 1)

            def step(n, h, s1, turn, s2):
                if s1:
                    pe.wait_ge(s_load[h], 96 * (n + 1))
                elif h == 0:
                    pe.wait_ge(s1_read.sem, s1_read.at(n, 0))
                    pe.sem_inc(s1_mm.sem, TURN)
                u = 0
                for slot, units in enumerate(SLOTS):
                    if s2 and slot < NT:
                        exp_unit(n, h, slot)
                    for u in range(u, u + units):
                        if u == TURN:
                            if turn:
                                turn_unit(n, h)
                            elif s1:
                                pe.wait_ge(s1_read.sem, s1_read.at(n, u))
                                pe.sem_inc(s1_mm.sem, 1)
                        elif s1:
                            max_unit(n, h, u)
                    u += 1
                    if s2 and slot >= 2:
                        value_unit(n, h, slot - 2)

            over_groups(pe, step)
            step(NG, 0, False, True, True)
            step(NG, 1, False, False, True)
            for b in range(NB):
                pe.wait_ge(s_scaled, b + 1)
                if b >= 2:
                    pe.wait_ge(s_added, b - 1)
                for h in range(2):
                    last = pe.matmul(s2_ps[b % 2][:, h * 512:(h + 1) * 512], Wo[:, :],
                                     OA[:, b % 2, h * 512:(h + 1) * 512], start=True, stop=True)
                last.then_inc(s_out_mm, 1)

        @block.scalar
        def _(act):
            norm.scalar(act)

            def split(b):
                for w in range(2):
                    act.wait_ge(rsum.sem, rsum.at(b, w + 1))
                    wait(act, s_parts_out[w], 16 * b)
                    act.activation(RP[:, w, 0, :], R[:, :], ACT.Copy).then_inc(p1.sem, 1)
                    act.wait_ge(r1.sem, r1.at(b, w + 1))
                    act.activation(RP[:, w, 1, :], R[:, :], ACT.Copy).then_inc(p2.sem, 1)

            over_sequences(act, split)

            def step(n, h, s1, turn, s2):
                if not s2:
                    return

                def copy_out(half):
                    act.wait_ge(pv.sem, pv.at(n, NT * (h - 2) + 4 * half + 4))
                    if half == 0:
                        wait(act, s_stored[h % 2], 32 * n + 16 * (h // 2 - 1))
                    act.activation(OS[:, h % 2, half * 512:(half + 1) * 512], o_ps[half][0:BD + 1, :], ACT.Copy)\
                       .then_inc(o_read.sem, 1)

                for j in range(NT):
                    width = T - j * P
                    act.wait_ge(s2_mm.sem, s2_mm.at(n, NT * (h - 2) + j + 1))
                    wait(act, pv.sem, pv.at(n, NT * (h - 2) + j - 3))
                    act.activation(PT[:, j % 4, 0:width], s2_ps[j % 2][:, 0:width], ACT.Exp).then_inc(probs.sem, 1)
                    if j == 6:
                        copy_out(0)
                copy_out(1)

            over_groups(act, step)
            step(NG, 0, False, True, True)
            step(NG, 1, False, False, True)

        @block.vector
        def _(dve):
            dve.memset(ones[:, :, :], 1.0).then_inc(s_set, 1)
            dve.memset(NX[:, :, 1, 0:4], 3e38)
            dve.memset(VB[:, :, :, :, :], 1.0).then_inc(s_set, 1)
            norm.vector(dve, lambda c, hc, rs: dve.tensor_tensor(XN[:, c // 2, c % 2 * 512:(c % 2 + 1) * 512],
                                                                 hc, rs, ALU.mult))
            dve.wait_ge(s_w, 16 * 9)
            dve.wait_ge(s_set, 2)

            def rotate(b):
                for w in range(2):
                    if w == 0:
                        wait(dve, p3.sem, p3.at(b, 0))
                    for i, dst in enumerate((T1, T2)):
                        dve.wait_ge(ab_mm.sem, ab_mm.at(b, 2 * w + i + 1))
                        wait(dve, rsum.sem, rsum.at(b, w))
                        for h in range(2):
                            half = slice(h * 512, (h + 1) * 512)
                            last = dve.tensor_tensor(dst[:, half], s2_ps[i][:, half], rope[:, 2 * w + i, half], ALU.mult)
                        last.then_inc(turned.sem, 1)
                    dve.wait_ge(turned.sem, turned.at(b, 2 * w + 2))
                    wait(dve, p3.sem, p3.at(b, w))
                    dve.tensor_tensor(R[:, :], T1[:, :], T2[:, :], ALU.add).then_inc(rsum.sem, 1)
                    dve.wait_ge(p1.sem, p1.at(b, w + 1))
                    dve.wait_ge(rsum.sem, rsum.at(b, w + 1))
                    dve.tensor_tensor(R[:, :], R[:, :], RP[:, w, 0, :], ALU.subtract).then_inc(r1.sem, 1)
                    dve.wait_ge(p2.sem, p2.at(b, w + 1))
                    dve.wait_ge(r1.sem, r1.at(b, w + 1))
                    dve.tensor_tensor(RP[:, w, 2, :], R[:, :], RP[:, w, 1, :], ALU.subtract).then_inc(p3.sem, 1)
                dve.wait_ge(v_mm.sem, v_mm.at(b, 1))
                for g in range(BH // BG):
                    for half in range(2):
                        v = s1_ps[half][:, :].rearrange("p (t g h e) -> p t g h e", t=4, g=BH // BG, h=BG)[:, :, g]
                        last = dve.tensor_copy(
                            VB[:, bass.ds(b * (BH // BG) + g, 1), 4 * half:4 * half + 4, :, 0:BD]
                            .rearrange("p a t h e -> p (a t) h e"), v)
                last.then_inc(v_copied.sem, 1)

            over_sequences(dve, rotate)
            dve.wait_ge(v_copied.sem, NB)

            def step(n, h, s1, turn, s2):
                if s1:
                    wait(dve, pv.sem, pv.at(n, NT * (h - 3)))
                    dve.tensor_copy(VQ[:, h, :, :], VB[:, bass.ds(n, 1), :, h, :].rearrange("p a t e -> p (a t) e"))\
                       .then_inc(vq.sem, 1)
                    wait(dve, parts.sem, parts.at(n, 4 * (h - 1)))
                elif h == 0:
                    dve.wait_ge(s1_mm.sem, s1_mm.at(n, TURN))
                    dve.sem_inc(s1_read.sem, TURN)
                for u in range(UNITS):
                    bank = s1_ps[(UNITS * h + u) % 2]
                    if u == TURN:
                        if turn:
                            k = (h - 1) % BG
                            dve.wait_ge(s1_mm.sem, s1_mm.at(n, UNITS * h + u + 1))
                            o = (h - 3) % BG
                            wait(dve, s_rows[o], 16 * (n + 1 + (h - 3 - o) // BG))
                            dve.tensor_copy(MT[:, k % 2, :], bank[0:PARTS * NT, 0:P]).then_inc(s1_read.sem, 1)
                        elif s1:
                            dve.wait_ge(s1_mm.sem, s1_mm.at(n, u + 1))
                            dve.sem_inc(s1_read.sem, 1)
                    elif s1:
                        i, c = CHUNKS[u if u < TURN else u - 1]
                        lo, hi = chunk_keys(i, c)
                        dve.wait_ge(s1_mm.sem, s1_mm.at(n, UNITS * h + u + 1))
                        dve.tensor_reduce(NX[:, h % 2, c, i:i + 1], bank[:, 0:hi - lo], AX_X, ALU.max, negate=True)\
                           .then_inc(s1_read.sem, 1)
                if s1:
                    dve.wait_ge(s1_read.sem, s1_read.at(n, UNITS * (h + 1)))
                    dve.tensor_tensor(NM[:, h % 2, :], NX[:, h % 2, 0, :], NX[:, h % 2, 1, :], ALU.min)\
                       .then_inc(maxima.sem, 1)

            over_groups(dve, step)
            step(NG, 0, False, True, True)
            for b in range(NB):
                dve.wait_ge(s_back[b % 2], 32 * (b // 2 + 1))
                dve.reciprocal(DA[:, b % 2, :], DA[:, b % 2, :]).then_inc(s_rden, 1)
                dve.wait_ge(s_rden, b + 1)
                dve.tensor_tensor(OA[:, b % 2, :], OA[:, b % 2, :], DA[:, b % 2, :], ALU.mult).then_inc(s_scaled, 1)
                dve.wait_ge(s_out_mm, b + 1)
                x = X[:, b * T:(b + 1) * T]
                for h in range(2):
                    x = X[:, b * T + h * 512:b * T + (h + 1) * 512]
                    last = dve.tensor_tensor(x, s2_ps[b % 2][:, h * 512:(h + 1) * 512], x, ALU.add)
                last.then_inc(s_added, 1)
            dve.wait_ge(s_added, NB)

        @block.gpsimd
        def _(pool):
            pool.memset(zeros[:, :], 0.0).then_inc(s_zeros, 1)
            pool.wait_ge(norm.s_out, norm.chunks)

            def fetch(b):
                wait(pool, v_mm.sem, v_mm.at(b, 0))
                pool.tensor_copy(XB[:, :], XN[:, bass.ds(b, 1), :].rearrange("p a t -> p (a t)")).then_inc(xb.sem, 1)

            over_sequences(pool, fetch)

            pool.wait_ge(s_zeros, 1)

            def step(n, h, s1, turn, s2):
                i = h % 2
                pool.wait_ge(maxima.sem, maxima.at(n, h + 1))
                wait(pool, s1_mm.sem, s1_mm.at(n, UNITS * (h - 1) + TURN + 1))
                nm, nr = NM[:, i, :], NR[:, i, :]
                part = lambda a: NP[:, i, a, :]
                done = lambda k: pool.wait_ge(parts.sem, parts.at(n, 4 * h + k))
                pool.tensor_tensor(part(0), nm, zeros[:, :], ALU.add).then_inc(parts.sem, 1)
                done(1)
                pool.tensor_tensor(nr, nm, part(0), ALU.subtract).then_inc(parts.sem, 1)
                done(2)
                pool.tensor_tensor(part(1), nr, zeros[:, :], ALU.add).then_inc(parts.sem, 1)
                done(3)
                pool.tensor_tensor(part(2), nr, part(1), ALU.subtract).then_inc(parts.sem, 1)

            over_groups(pool, step)


def output_stage(nc, out, keep):
    X, ident = keep["X"], keep["ident"]
    with nc.cleanup_on_exit(), ExitStack() as ctx:
        sb, ps, sem = allocators(nc, ctx, "out_")
        O = sb("O", [P, NB * NT, P])
        bank = [ps(f"bank{i}", [P, 512]) for i in range(4)]
        s_turned, s_copied, s_stored = sem("turned"), sem("copied"), sem("stored")
        N = NB * NT // 4
        block = ctx.enter_context(nc.Block())

        @block.tensor
        def _(pe):
            for n in range(N):
                if n >= 4:
                    pe.wait_ge(s_copied, n - 3)
                for i in range(4):
                    at = (4 * n + i) * P
                    last = pe.transpose(bank[n % 4][:, i * P:(i + 1) * P], X[:, at:at + P], ident[:, :])
                last.then_inc(s_turned, 1)

        @block.vector
        def _(dve):
            for n in range(N):
                dve.wait_ge(s_turned, n + 1)
                dve.tensor_copy(O[:, 4 * n:4 * n + 4, :].rearrange("p t c -> p (t c)"), bank[n % 4][:, :])\
                   .then_inc(s_copied, 1)

        @block.sync
        def _(sp):
            for n in range(N):
                sp.wait_ge(s_copied, n + 1)
                b, t = n // 2, n % 2 * 4
                sp.dma_start(out[b, t * P:(t + 4) * P, :].rearrange("(t p) c -> p t c", p=P),
                             O[:, 4 * n:4 * n + 4, :]).then_inc(s_stored, 16)
            sp.wait_ge(s_stored, 16 * N)


def network(nc, d, out):
    part = lambda name: {k[len(name) + 1:]: v for k, v in d.items() if k.startswith(name + "_")}
    shared = part("shared")
    with ExitStack() as ctx:
        sb = lambda name, shape, dt=F32: ctx.enter_context(nc.sbuf_tensor(name, shape, dt))
        keep = {"X": sb("X", [P, NB * T]), "ident": sb("ident", [P, P]), "identb": sb("identb", [P, P], BF16),
                "mean": sb("mean", [P, P]), "centre": sb("centre", [P, P]), "eps": sb("eps", [P, 1])}
        attn_a_stage(nc, {**shared, **part("attn_a")}, keep)
        ffn_stage(nc, {**shared, **part("ffn")}, keep, 0)
        attn_b_stage(nc, {**shared, **part("attn_b")}, keep)
        ffn_stage(nc, {**shared, **part("ffn")}, keep, 1)
        output_stage(nc, out, keep)


def causal_masks(np):
    low = np.tril(np.ones((P, P), bool))
    return np.where(np.stack([low, low.T], 1), 0.0, -3e38)


def band_masks(np):
    q = np.arange(P)[:, None]
    k = np.arange(P)[None, :] - WIN + q // WIN * WIN
    m = np.repeat(np.where((k <= q) & (q <= k + WIN), 0.0, -3e38)[:, None, :], NT, 1)
    m[:, 0, :] = np.where(k >= 0, m[:, 0, :], -3e38)
    return m


def xpos_tables(np):
    half = np.arange(0, DH, 2, dtype=np.float32)
    inv_freq = np.float32(1.0) / np.float32(10000.0) ** (half / np.float32(DH))
    t = np.arange(T, dtype=np.float32)
    freqs = (t[:, None] * inv_freq[None, :]).astype(np.float64)
    base = ((half + np.float32(0.4 * DH)) / np.float32(1.4 * DH)).astype(np.float64)
    scale = base[None, :] ** ((t - T // 2) / (WIN // 2)).astype(np.float64)[:, None]
    out = np.zeros((2, T, 2, DH))
    for i, s in enumerate((8.0 * scale, 1.0 / scale)):
        out[0, :, i] = np.concatenate([np.cos(freqs) * s] * 2, 1)
        out[1, :, i] = np.concatenate([-np.sin(freqs) * s, np.sin(freqs) * s], 1)
    return out.reshape(2, NT, P, 2, DH).transpose(0, 2, 1, 3, 4).astype(np.float32)


def rope_tables(np):
    dim = np.arange(0, BD, 2, dtype=np.float32)
    inv_freq = np.float32(1.0) / np.float32(10000.0) ** (dim / np.float32(BD))
    angle = (np.arange(T, dtype=np.float32)[None, :] * inv_freq[:, None]).astype(np.float64)
    angle = np.tile(np.repeat(angle, 2, 0), (BH, 1))
    sign = np.where(np.arange(P) % 2, 1.0, -1.0)[:, None]
    cos, sin = np.cos(angle), np.sin(angle) * sign
    s = 1.0 / np.sqrt(np.float64(BD))
    return np.stack([cos * s, sin * s, cos, sin], 1).astype(np.float32)


def kernel(**inputs):
    import ml_dtypes
    import numpy as np
    import concourse.bacc as bacc
    from concourse.bass_utils import run_bass_kernel_spmd

    a = {name[len("L0_"):]: np.ascontiguousarray(value) for name, value in inputs.items()}
    tiles = lambda v: v.reshape(CT, P).T
    column = lambda v: v.reshape(P, 1)
    pairs = np.arange(P) ^ 1
    bf16 = ml_dtypes.bfloat16
    arrays = {
        "shared_ident": np.eye(P, dtype=np.float32),
        "shared_identb": np.eye(P, dtype=np.float32).astype(bf16),
        "shared_mean": np.full((P, P), 1.0 / P, np.float32),
        "shared_centre": (np.eye(P) - 1.0 / P).astype(np.float32),
        "shared_eps": np.full((P, 1), EPS, np.float32),
        "attn_a_x": a["attn_a_x"],
        "attn_a_pos": np.arange(T, dtype=np.float32).reshape(1, T),
        "attn_a_shift": np.full((P, 1), 10 * math.log(2), np.float32),
        "attn_a_heads16": np.kron(np.eye(P // 16), np.ones((16, 16))).astype(np.float32),
        "attn_a_freqs": tiles(a["attn_a_freqs"]),
        "attn_a_gamma": tiles(np.repeat(a["attn_a_gamma"].reshape(16), 16)),
        "attn_a_conv_w": a["attn_a_conv_w"].reshape(P, 4),
        "attn_a_conv_b": column(a["attn_a_conv_b"]),
        "attn_a_qk_wT": a["attn_a_qk_w"].T,
        "attn_a_v_wT": a["attn_a_v_w"].T,
        "attn_a_g_wT": a["attn_a_g_w"].T,
        "attn_a_o_wT": a["attn_a_o_w"].T,
        "attn_a_g_b": tiles(a["attn_a_g_b"]),
        "attn_a_ln_g": column(a["attn_a_ln_g"]),
        "attn_a_ln_b": column(a["attn_a_ln_b"]),
        "ffn_band": band_masks(np).astype(bf16),
        "ffn_rope": xpos_tables(np),
        "attn_b_causal": causal_masks(np).astype(bf16),
        "attn_b_rope": rope_tables(np),
        "attn_b_WqT": a["attn_b_Wq"].T,
        "attn_b_WqpT": a["attn_b_Wq"][pairs].T,
        "attn_b_WkT": a["attn_b_Wk"].T,
        "attn_b_WkpT": a["attn_b_Wk"][pairs].T,
        "attn_b_WvT": a["attn_b_Wv"].T,
        "attn_b_WoT": a["attn_b_Wo"].T,
    }
    for name in ("wqkv", "q_scale", "k_scale", "wo", "ln_g", "ln_b", "w1", "b1", "w2", "b2"):
        arrays["ffn_" + name] = a["ffn_" + name]

    nc = bacc.Bacc("TRN2", target_bir_lowering=False, num_devices=1)
    d, feeds = {}, {}
    for name, value in arrays.items():
        feeds[f"in_{name}_dram"] = np.ascontiguousarray(value)
        d[name] = nc.dram_tensor(f"in_{name}_dram", value.shape, mybir.dt.from_np(value.dtype),
                                 kind="ExternalInput").ap()
    out = nc.dram_tensor("out_0_dram", (NB, T, P), F32, kind="ExternalOutput").ap()
    network(nc, d, out)
    return run_bass_kernel_spmd(nc, [feeds], core_ids=[0]).results[0]["out_0_dram"]
```

```python
import math
from contextlib import ExitStack

import concourse.bass as bass
from concourse import mybir

P = 128
NB, T = 4, 1024
NT = T // P
PAD = 4
EPS = 1e-5
F32 = mybir.dt.float32
BF16 = mybir.dt.bfloat16
ALU = mybir.AluOpType
ACT = mybir.ActivationFunctionType
AX_X = mybir.AxisListType.X

DEPTH = 2
NH, DH = 8, 64
INNER = NH * DH
NPAIR = NH // 2
WIN = 64
WK = P + WIN
HID_DIM = P * 4 * 2 // 3
NHC = 3
HC = -(-HID_DIM // NHC)
QUAD = 4
NQ = NH // QUAD
NSTEP = NB * NQ
LAG = 3
PR = 4

CT = 2
TABLES = 1 + 10 * CT + 2

BH, BD = 16, 8
BG = 4
NG = NB * BH // BG
PARTS = 3
KS9 = PARTS * PARTS * BD

class Count:

    def __init__(self, sem, per, credit=0):
        self.sem, self.per, self.credit = sem, per, credit

    def at(self, g, k):
        return g * self.per + (self.credit + k)


def allocators(nc, ctx, prefix):
    def sb(name, shape, dt=F32):
        return ctx.enter_context(nc.sbuf_tensor(prefix + name, shape, dt))

    def ps(name, shape, dt=F32):
        return ctx.enter_context(nc.psum_tensor(prefix + name, shape, dt))

    def sem(name):
        return nc.alloc_semaphore(prefix + name)

    return sb, ps, sem


class Norm:

    def __init__(self, sem, keep, chunks, banks, dst, rs, sq):
        self.keep, self.chunks, self.banks = keep, chunks, banks
        self.dst, self.rs, self.sq = dst, rs, sq
        self.s_centred = sem("n_centred")
        self.s_squared = sem("n_squared")
        self.s_copied = sem("n_copied")
        self.s_var = sem("n_var")
        self.s_ln = sem("n_ln")
        self.s_rstd = sem("n_rstd")
        self.s_out = sem("n_out")

    def tensor(self, pe, source, ready=None):
        for c in range(self.chunks + 1):
            if c < self.chunks:
                if ready:
                    ready(pe, c)
                if c >= 2:
                    pe.wait_ge(self.s_copied, c - 1)
                pe.matmul(self.banks[c % 2][:, :], self.keep["centre"][:, :], source(c),
                          start=True, stop=True).then_inc(self.s_centred, 1)
            if c >= 1:
                v = c - 1
                pe.wait_ge(self.s_squared, v + 1)
                if v >= 2:
                    pe.wait_ge(self.s_ln, v - 1)
                pe.matmul(self.banks[2 + v % 2][:, :], self.keep["mean"][:, :], self.sq[:, v % 2, :],
                          start=True, stop=True).then_inc(self.s_var, 1)

    def scalar(self, act):
        for c in range(self.chunks + 1):
            if c < self.chunks:
                act.wait_ge(self.s_copied, c + 1)
                if c >= 2:
                    act.wait_ge(self.s_var, c - 1)
                act.activation(self.sq[:, c % 2, :], self.dst(c), ACT.Square).then_inc(self.s_squared, 1)
            if c >= 1:
                v = c - 1
                act.wait_ge(self.s_var, v + 1)
                act.activation(self.rs(v), self.banks[2 + v % 2][:, :], ACT.Ln,
                               bias=self.keep["eps"][:, :]).then_inc(self.s_ln, 1)
        for c in range(self.chunks):
            act.wait_ge(self.s_ln, self.chunks)
            act.activation(self.rs(c), self.rs(c), ACT.Exp, scale=-0.5).then_inc(self.s_rstd, 1)

    def vector(self, dve):
        for c in range(self.chunks):
            dve.wait_ge(self.s_centred, c + 1)
            dve.tensor_copy(self.dst(c), self.banks[c % 2][:, :]).then_inc(self.s_copied, 1)
        for c in range(self.chunks):
            dve.wait_ge(self.s_squared, self.chunks)
            dve.wait_ge(self.s_rstd, c + 1)
            dve.tensor_tensor(self.dst(c), self.dst(c), self.rs(c), ALU.mult).then_inc(self.s_out, 1)


def half_columns(buffer, pad=0):
    return lambda c: buffer[:, c // 2, pad + c % 2 * 512:pad + (c % 2 + 1) * 512]


def ffn_stage(nc, d, keep, stage):
    X, ident = keep["X"], keep["ident"]
    with nc.cleanup_on_exit(), ExitStack() as ctx:
        sb, ps, sem = allocators(nc, ctx, f"ffn{stage}_")

        Y = sb("Y", [P, 2, NB, PAD + T])
        U = sb("U", [P, NB, PAD + T])
        Wqkv = sb("Wqkv", [P, 3, INNER])
        Wo = sb("Wo", [P, NPAIR, P])
        W1 = sb("W1", [P, 2, NHC, HC])
        W2 = sb("W2", [HC, NHC, P])
        B1 = sb("B1", [HC, 2, NHC])
        COLS = sb("COLS", [P, 3])
        QS = sb("QS", [P, 2, DH])
        rope = sb("rope", [P, 2, NT, 2, DH])
        masks = sb("masks", [P, NT, P], BF16)
        H1 = sb("H1", [P, NB, P])
        RAW = sb("RAW", [P, 2, 2, NH, DH])
        SQ = sb("SQ", [P, 2, NH, DH])
        SS = sb("SS", [P, 2 * NH])
        SC = sb("SC", [P, 2, 2 * NH])
        RN = sb("RN", [P, 2, 2 * NH])
        mhalf = sb("mhalf", [P, 2 * NH])
        T1 = sb("T1", [P, 2, 2, NH, DH])
        T2 = sb("T2", [P, 2, 2, NH, DH])
        QK = sb("QK", [P, 2, NPAIR, P])
        QT = sb("QT", [P, 2, NPAIR, 2, P])
        KT = sb("KT", [P, NB, NPAIR, WK])
        Vcur = sb("Vcur", [P, NB, INNER])
        Voff = sb("Voff", [P, NB, INNER])
        NM = sb("NM", [P, PR, QUAD])
        DEN = sb("DEN", [P, PR, QUAD])
        RDEN = sb("RDEN", [P, PR, QUAD])
        PB = sb("PB", [P, PR, QUAD, P])
        PT = sb("PT", [P, 2, QUAD, P])
        OT = sb("OT", [P, NPAIR, NB, P])
        H2 = sb("H2", [P, NB, P])
        HC2, SQ2, RS, HN = (sb(name, [P, NB * P]) for name in ("HC2", "SQ2", "RS", "HN"))
        AG = sb("AG", [HC, 2, NHC, NB * P])
        proj_ps = [ps(f"proj{i}", [P, 512]) for i in range(2)]
        score_ps = [ps(f"score{i}", [P, 512]) for i in range(2)]
        turn_ps = [ps(f"turn{i}", [P, 512]) for i in range(2)]
        mlp_ps = [ps(f"mlp{i}", [P, 512]) for i in range(2)]
        norm = Norm(sem, keep, NB * T // 512, [proj_ps[0], proj_ps[1], score_ps[0], score_ps[1]],
                    dst=half_columns(Y[:, 0], PAD), rs=half_columns(U, PAD),
                    sq=T1[:, 0, :, :, :].rearrange("p c h k -> p c (h k)"))

        s_const, s_attn_w, s_mlp_w, s_zero, s_pads, s_scaled, s_added = (
            sem(n) for n in ("const", "attn_w", "mlp_w", "zero", "pads", "scaled", "added"))
        s_half = sem("half")
        count = lambda name, per, credit=0: Count(sem(name), per, credit)
        h1_low, h1_high = count("h1_low", 1), count("h1_high", 1)
        qk_proj, v_proj = count("qk_proj", 2 * NB), count("v_proj", NB, 1)
        raw = count("raw", 2 * NB)
        sumsq, clamped, rnorm = count("sumsq", NB, 1), count("clamped", NB, 1), count("rnorm", NB, 2)
        roped, rope_sum, qk = count("roped", NB, 2), count("rope_sum", NB, 1), count("qk", NB, 2)
        qk_turned = count("qk_turned", 2 * NB, 1)
        qt, kshift, kt = count("qt", NB, 2), count("kshift", NB), count("kt", NB, NB)
        vshift, v_ready = count("vshift", NB), count("v_ready", NB, NB)
        v_read = count("v_read", NB, NB)
        scores, negmax, probs = count("scores", NSTEP, NSTEP), count("negmax", NSTEP), count("probs", NSTEP, 2)
        rden, normed = count("rden", NSTEP), count("normed", NSTEP)
        p_turned, pt = count("p_turned", NSTEP, PR), count("pt", NSTEP)
        o, ot = count("o", NSTEP, NSTEP), count("ot", NSTEP, 2)
        MLP_MM = 3 + 2 * NHC + 1
        mlp_mm = count("mlp_mm", MLP_MM, MLP_MM)
        u, h2 = count("u", 1), count("h2", 1)
        centred, squared = count("centred", 1), count("squared", 1)
        lnvar, rstd, hn = count("lnvar", 1), count("rstd", 1), count("hn", 2)
        gate, value = count("gate", NHC, 1), count("value", NHC)
        gelu, hid, ynext = count("gelu", NHC), count("hid", NHC), count("ynext", 1, NT)

        PROJ_USE = [("q", 2), ("k", 2), ("v", 2), ("qt", 1), ("kt", 1)]

        def proj_use(kind, b):
            place = next(i for i, use in enumerate(PROJ_USE) if use[0] == kind)
            return len(PROJ_USE) * (b - PROJ_USE[place][1]) + place

        def proj_bank(kind, b):
            return proj_ps[proj_use(kind, b) % 2]

        def wait_proj_bank(pe, kind, b, g):
            step, place = divmod(proj_use(kind, b) - 2, len(PROJ_USE))
            was, ahead = PROJ_USE[place]
            c = step + ahead
            if was in "qk":
                pe.wait_ge(raw.sem, raw.at(g, 2 * c + 1 + "qk".index(was)))
            elif was == "v":
                pe.wait_ge(v_read.sem, v_read.at(g, c + 1))
            elif was == "qt":
                pe.wait_ge(qt.sem, qt.at(g, c + 1))
            else:
                pe.wait_ge(kt.sem, kt.at(g, c + 1))

        N_ATTN_LOADS, N_MLP_LOADS = 3, 5

        MLP_AT = {(1, 0): 0, (1, 1): 1, (2, 0): 2, (3, 0): 3, (3, 1): 4}
        MLP_LAST = 5

        def groups(eng, enter, attention, quad, mlp, mlp_at=MLP_AT):
            def run(g, t, l, now, before, ahead, finish=True):
                for b in range(NB):
                    for r in range(NQ):
                        for name, to in ((("proj_qk", b + 2), ("quad", 0), ("rotate", b + 1), ("proj_v", b + 2),
                                          ("norms", b + 2), ("turn", b + 1), ("v_off", b + 2)),
                                         (("quad", 0), ("sum", b + 2)))[r]:
                            if name == "quad":
                                if now or NQ * b + r < LAG:
                                    quad(NQ * b + r, g, t, now, before)
                            elif to < NB and now:
                                alone = name == "turn" and b + 2 >= NB and not ahead
                                attention("turn_alone" if alone else name, to, g, t, l)
                            elif to >= NB and ahead:
                                attention(name, to - NB, g + 1, t + 1, l)
                        if (b, r) == (1, 0) and ahead:
                            attention("h1", 0, g + 1, t + 1, l)
                        if before and mlp and (b, r) in mlp_at:
                            mlp(mlp_at[b, r], g - 1, t - 1, l)
                        if finish and mlp and (b, r) == (0, 0):
                            mlp(MLP_LAST, g - 2, t - 2, l)

            with eng.Fori(0, DEPTH) as l:
                enter(l)
                g = l * NT
                attention("h1", 0, g, 0, l)
                attention("proj_qk", 0, g, 0, l)
                attention("proj_v", 0, g, 0, l)
                attention("v_off", 0, g, 0, l)
                attention("norms", 0, g, 0, l)
                attention("sum", 0, g, 0, l)
                attention("first", 0, g, 0, l)
                attention("rotate", 0, g, 0, l)
                attention("proj_qk", 1, g, 0, l)
                attention("proj_v", 1, g, 0, l)
                attention("v_off", 1, g, 0, l)
                attention("turn", 0, g, 0, l)
                attention("norms", 1, g, 0, l)
                attention("sum", 1, g, 0, l)
                run(g, 0, l, True, False, True, finish=False)
                run(g + 1, 1, l, True, True, True, finish=False)
                with eng.Fori(2, NT - 1) as t:
                    run(l * NT + t, t, l, True, True, True)
                run(l * NT + NT - 1, NT - 1, l, True, True, False)
                run(l * NT + NT, NT, l, False, True, False)
                if mlp:
                    mlp(MLP_LAST, l * NT + NT - 1, NT - 1, l)

        def cols(t, late=0):
            return bass.ds(t * P + (PAD - late), P)


        block = ctx.enter_context(nc.Block())

        @block.sync
        def _(sp):
            sp.dma_start(masks[:, :, :], d["band"]).then_inc(s_const, 16)
            with sp.Fori(0, DEPTH) as l:
                layer = bass.ds(l, 1)

                sp.wait_ge(v_proj.sem, v_proj.at(l * NT, 0))
                sp.wait_ge(rope_sum.sem, rope_sum.at(l * NT, 0))
                sp.dma_start(Wqkv[:, :, :], d["wqkv"][layer].rearrange("a k (c n) -> k (a c) n", c=3))\
                  .then_inc(s_attn_w, 16)
                sp.dma_start(QS[:, :, :], d["scales"][layer].broadcast_to([P, 2, DH])).then_inc(s_attn_w, 16)
                sp.dma_start(rope[:, :, :, :, :], d["rope"].rearrange("k p t c e -> p k t c e")).then_inc(s_attn_w, 16)
                sp.wait_ge(ynext.sem, ynext.at(l * NT - 1, 1))
                sp.dma_start(Wo[:, :, :], d["wo"][layer].rearrange("a (q k) n -> k (a q) n", k=P)).then_inc(s_mlp_w, 16)
                sp.dma_start(W1[:, :, :, :], d["w1"][layer].rearrange("a k h j n -> k (a h) j n")).then_inc(s_mlp_w, 16)
                sp.dma_start(B1[:, :, :], d["b1"][layer].rearrange("a n h j -> n (a h) j")).then_inc(s_mlp_w, 16)
                sp.dma_start(W2[:, :, :], d["w2"][layer].rearrange("a k j n -> k (a j) n")).then_inc(s_mlp_w, 16)
                sp.dma_start(COLS[:, :], d["columns"][layer].rearrange("a p n -> p (a n)")).then_inc(s_mlp_w, 16)

        @block.tensor
        def _(pe):
            norm.tensor(pe, lambda c: X[:, c * 512:(c + 1) * 512])
            pe.wait_ge(s_const, 16)
            pe.sem_inc(scores.sem, scores.credit)
            pe.sem_inc(v_proj.sem, v_proj.credit)
            pe.sem_inc(qk_turned.sem, qk_turned.credit)
            pe.sem_inc(p_turned.sem, p_turned.credit)
            pe.sem_inc(o.sem, o.credit)
            pe.sem_inc(mlp_mm.sem, mlp_mm.credit)

            def enter(l):
                pe.wait_ge(s_attn_w, (l + 1) * (16 * N_ATTN_LOADS))

            def attention(name, n, g, t, l):
                if name in ("proj_qk", "proj_v"):
                    b = n
                    if b == 0 and name == "proj_qk":
                        pe.wait_ge(h1_low.sem, h1_low.at(g, 1))
                        pe.wait_ge(h1_high.sem, h1_high.at(g, 1))
                    for c, kind in ((0, "q"), (1, "k")) if name == "proj_qk" else ((2, "v"),):
                        wait_proj_bank(pe, kind, b, g)
                        done = v_proj if kind == "v" else qk_proj
                        pe.matmul(proj_bank(kind, b)[:, :], H1[:, b, :], Wqkv[:, c, :], start=True, stop=True)\
                          .then_inc(done.sem, 1)
                if name == "first":
                    pe.wait_ge(raw.sem, raw.at(g, 2))
                    pe.wait_ge(v_read.sem, v_read.at(g, 1))
                if name in ("turn", "turn_alone"):
                    b = n
                    pe.wait_ge(qk.sem, qk.at(g, b + 1))
                    for c, kind in enumerate(("qt", "kt")):
                        if name == "turn":
                            wait_proj_bank(pe, kind, b, g)
                        else:
                            was = (kt, qt)[c]
                            pe.wait_ge(was.sem, was.at(g, b))
                        bank = proj_bank(kind, b)
                        for p in range(NPAIR):
                            last = pe.transpose(bank[:, p * P:(p + 1) * P], QK[:, c, p, :], ident[:, :])
                        last.then_inc(qk_turned.sem, 1)

            def quad(n, g, t, now, before):
                if now:
                    s, b, r = n, n // NQ, n % NQ
                    if r == 0:
                        pe.wait_ge(qt.sem, qt.at(g, b + 1))
                        pe.wait_ge(kt.sem, kt.at(g, b + 1))
                    pe.wait_ge(probs.sem, probs.at(g, s - 1))
                    bank = score_ps[s % 2]
                    mask = masks[:, bass.ds(t, 1), :].broadcast_to([P, QUAD, P])
                    pe.matmul(bank[:, :], keep["identb"][:, :], mask, start=True, stop=True)
                    for i in range(QUAD):
                        p, e = (r * QUAD + i) // 2, i % 2
                        for w in range(2):
                            rows = slice(w * WIN, (w + 1) * WIN)
                            last = pe.matmul(bank[rows, i * P:(i + 1) * P], QT[:, b % 2, p, e, rows],
                                             KT[:, b, p, w * WIN:w * WIN + P], start=False,
                                             stop=True, skip_group_check=True)
                    last.then_inc(scores.sem, 1)
                s = n - (LAG - 1)
                if now if s >= 0 else before:
                    pe.wait_ge(normed.sem, normed.at(g, s + 1))
                    pe.wait_ge(ot.sem, ot.at(g, s - 1))
                    for i in range(QUAD):
                        last = pe.transpose(turn_ps[s % 2][:, i * P:(i + 1) * P], PB[:, s % PR, i, :], ident[:, :])
                    last.then_inc(p_turned.sem, 1)
                s = n - LAG
                if now if s >= 0 else before:
                    b, r = s % NSTEP // NQ, s % NQ
                    pe.wait_ge(pt.sem, pt.at(g, s + 1))
                    if r == 0:
                        pe.wait_ge(v_ready.sem, v_ready.at(g, s // NQ + 1))
                    for i in range(QUAD):
                        head, e = r * QUAD + i, i % 2
                        for w, V in enumerate((Voff, Vcur)):
                            at = (i // 2) * P + w * WIN
                            last = pe.matmul(turn_ps[s % 2][e * DH:(e + 1) * DH, at:at + WIN],
                                             V[:, b, head * DH:(head + 1) * DH],
                                             PT[:, s % 2, i, w * WIN:(w + 1) * WIN], start=True, stop=True)
                    last.then_inc(o.sem, 1)

            def mlp(n, g, t, l):
                bank = mlp_ps
                if n == 0:
                    pe.wait_ge(ot.sem, ot.at(g, NSTEP))
                    pe.wait_ge(s_mlp_w, (l + 1) * (16 * N_MLP_LOADS))
                    pe.wait_ge(gate.sem, gate.at(g - 1, NHC))
                    for p in range(NPAIR):
                        last = pe.matmul(bank[0][:, :], Wo[:, p, :], OT[:, p, :, :], start=(p == 0),
                                         stop=(p == NPAIR - 1))
                    last.then_inc(mlp_mm.sem, 1)
                if n == 1:
                    pe.wait_ge(h2.sem, h2.at(g, 1))
                    pe.wait_ge(ynext.sem, ynext.at(g - 1, 1))
                    pe.matmul(bank[1][:, :], keep["centre"][:, :], H2[:, :, :], start=True, stop=True)\
                      .then_inc(mlp_mm.sem, 1)
                if n == 2:
                    pe.wait_ge(squared.sem, squared.at(g, 1))
                    pe.wait_ge(u.sem, u.at(g, 1))
                    pe.matmul(bank[0][:, :], keep["mean"][:, :], SQ2[:, :], start=True, stop=True)\
                      .then_inc(mlp_mm.sem, 1)
                if n in (3, 4):
                    for j in range(0, 1) if n == 3 else range(1, NHC):
                        if j == 0:
                            pe.wait_ge(hn.sem, hn.at(g, 2))
                            pe.wait_ge(centred.sem, centred.at(g, 1))
                            pe.wait_ge(lnvar.sem, lnvar.at(g, 1))
                        else:
                            pe.wait_ge(value.sem, value.at(g, j))
                        pe.matmul(bank[1][0:HC, :], W1[:, 0, j, :], HN[:, :], start=True, stop=True)\
                          .then_inc(mlp_mm.sem, 1)
                        if j:
                            pe.wait_ge(gate.sem, gate.at(g, j))
                        pe.matmul(bank[0][0:HC, :], W1[:, 1, j, :], HN[:, :], start=True, stop=True)\
                          .then_inc(mlp_mm.sem, 1)
                if n == 5:
                    pe.wait_ge(value.sem, value.at(g, NHC))
                    for j in range(NHC):
                        pe.wait_ge(hid.sem, hid.at(g, j + 1))
                        last = pe.matmul(bank[1][:, :], W2[:, j, :], AG[:, 0, j, :], start=(j == 0),
                                         stop=(j == NHC - 1))
                    last.then_inc(mlp_mm.sem, 1)

            groups(pe, enter, attention, quad, mlp)

        @block.scalar
        def _(act):
            norm.scalar(act)
            act.sem_inc(qt.sem, qt.credit)
            act.sem_inc(v_ready.sem, v_ready.credit)
            act.sem_inc(v_read.sem, v_read.credit)
            act.sem_inc(probs.sem, probs.credit)
            act.sem_inc(ot.sem, ot.credit)
            act.wait_ge(norm.s_out, norm.chunks)
            act.wait_ge(s_zero, 4)
            act.wait_ge(s_pads, 2)
            enter = lambda l: None

            def attention(name, n, g, t, l):
                if name == "h1":
                    act.wait_ge(ynext.sem, ynext.at(g - NT, 1))
                    act.wait_ge(v_proj.sem, v_proj.at(g, 0))
                    act.activation(H1[64:P, :, :], Y[64:P, bass.ds(l, 1), :, cols(t, 1)]
                                   .rearrange("p a b c -> p (a b) c"), ACT.Copy).then_inc(h1_high.sem, 1)
                if name == "proj_qk":
                    b = n
                    act.wait_ge(sumsq.sem, sumsq.at(g, b))
                    act.wait_ge(roped.sem, roped.at(g, b - 1))
                    for c in range(2):
                        act.wait_ge(qk_proj.sem, qk_proj.at(g, 2 * b + c + 1))
                        bank = proj_bank("qk"[c], b)[:, :].rearrange("p (h e) -> p h e", e=DH)
                        act.activation(SQ[:, c, :, :], bank, ACT.Square)
                        act.activation(RAW[:, b % 2, c, :, :], bank, ACT.Copy).then_inc(raw.sem, 1)
                if name == "proj_v":
                    b = n
                    act.wait_ge(v_proj.sem, v_proj.at(g, b + 1))
                    act.wait_ge(vshift.sem, vshift.at(g, b + 1))
                    bank = proj_bank("v", b)
                    act.activation(Vcur[:, b, :], bank[:, :], ACT.Copy).then_inc(v_read.sem, 1)
                if name == "v_off":
                    b = n
                    act.wait_ge(v_read.sem, v_read.at(g, b + 1))
                    act.activation(Voff[WIN:P, b, :], Vcur[0:WIN, b, :], ACT.Copy).then_inc(v_ready.sem, 1)
                if name in ("turn", "turn_alone"):
                    b = n
                    act.wait_ge(qk_turned.sem, qk_turned.at(g, 2 * b + 1))
                    act.wait_ge(scores.sem, scores.at(g, NQ * (b - 1)))
                    bank = proj_bank("qt", b)[:, :].rearrange("p (q c) -> p q c", q=NPAIR)
                    act.activation(QT[0:DH, b % 2, :, 0, :], bank[0:DH], ACT.Copy)
                    act.activation(QT[DH:P, b % 2, :, 1, :], bank[DH:P], ACT.Copy).then_inc(qt.sem, 1)

            def quad(n, g, t, now, before):
                if now:
                    s = n
                    act.wait_ge(negmax.sem, negmax.at(g, s + 1))
                    act.wait_ge(p_turned.sem, p_turned.at(g, s - PR + 1))
                    for i in range(QUAD):
                        last = act.activation(PB[:, s % PR, i, :], score_ps[s % 2][:, i * P:(i + 1) * P],
                                              ACT.Exp, bias=NM[:, s % PR, i:i + 1],
                                              accum_out=DEN[:, s % PR, i:i + 1])
                    last.then_inc(probs.sem, 1)
                s = n - LAG
                if now if s >= 0 else before:
                    act.wait_ge(o.sem, o.at(g, s + 1))
                    if s == 0:
                        act.wait_ge(mlp_mm.sem, mlp_mm.at(g - 1, 1))
                    b, p = s % NSTEP // NQ, (s % NQ) * QUAD // 2
                    act.activation(OT[:, p:p + QUAD // 2, b, :],
                                   turn_ps[s % 2][:, 0:QUAD // 2 * P].rearrange("p (q c) -> p q c", c=P),
                                   ACT.Copy).then_inc(ot.sem, 1)

            def mlp(n, g, t, l):
                if n == 0:
                    act.wait_ge(u.sem, u.at(g, 1))
                    act.activation(H2[0:64, :, :], U[0:64, :, cols(t)], ACT.Copy)
                    act.activation(H2[64:P, :, :], U[64:P, :, cols(t, 1)], ACT.Copy).then_inc(h2.sem, 1)
                if n == 1:
                    act.wait_ge(centred.sem, centred.at(g, 1))
                    act.activation(SQ2[:, :], HC2[:, :], ACT.Square).then_inc(squared.sem, 1)
                if n == 2:
                    act.wait_ge(mlp_mm.sem, mlp_mm.at(g, 3))
                    act.activation(RS[:, :], mlp_ps[0][:, :], ACT.Ln, bias=keep["eps"][:, :]).then_inc(lnvar.sem, 1)
                    act.wait_ge(lnvar.sem, lnvar.at(g, 1))
                    act.activation(RS[:, :], RS[:, :], ACT.Exp, scale=-0.5).then_inc(rstd.sem, 1)
                if n == 3:
                    act.wait_ge(s_mlp_w, (l + 1) * (16 * N_MLP_LOADS))
                if n in (3, 4):
                    for j in range(0, 1) if n == 3 else range(1, NHC):
                        act.wait_ge(mlp_mm.sem, mlp_mm.at(g, 4 + 2 * j))
                        act.activation(AG[:, 0, j, :], mlp_ps[1][0:HC, :], ACT.Identity,
                                       bias=B1[:, 0, j:j + 1]).then_inc(value.sem, 1)
                if n == 4:
                    act.wait_ge(gate.sem, gate.at(g, NHC))
                    for j in range(NHC):
                        act.activation(AG[:, 1, j, :], AG[:, 1, j, :], ACT.Gelu).then_inc(gelu.sem, 1)

            groups(act, enter, attention, quad, mlp)

        @block.vector
        def _(dve):
            dve.memset(Y[:, :, :, 0:PAD], 0.0).then_inc(s_pads, 1)
            dve.memset(U[:, :, 0:PAD], 0.0).then_inc(s_pads, 1)
            norm.vector(dve)
            dve.wait_ge(s_zero, 4)
            dve.wait_ge(s_pads, 2)
            dve.wait_ge(norm.s_out, norm.chunks)
            for c in (sumsq, clamped, roped, qk, kt, gate, ynext):
                dve.sem_inc(c.sem, c.credit)

            def enter(l):
                dve.wait_ge(s_attn_w, (l + 1) * (16 * N_ATTN_LOADS))
                spread = lambda a: a.unsqueeze(1).broadcast_to([P, NT] + list(a.shape[1:]))
                dve.tensor_tensor(rope[:, 0, :, :, :], rope[:, 0, :, :, :], spread(QS[:, :, :]), ALU.mult)\
                   .then_inc(s_scaled, 1)
                for h in range(2):
                    a, b = slice(32 * h, 32 * h + 32), slice(32 - 32 * h, 64 - 32 * h)
                    dve.tensor_tensor(rope[:, 1, :, :, a], rope[:, 1, :, :, a], spread(QS[:, :, b]), ALU.mult)\
                       .then_inc(s_scaled, 1)
                dve.wait_ge(s_scaled, 3 * l + 3)

            def attention(name, n, g, t, l):
                if name == "h1":
                    dve.wait_ge(ynext.sem, ynext.at(g - NT, 1))
                    dve.wait_ge(v_proj.sem, v_proj.at(g, 0))
                    dve.tensor_copy(H1[0:64, :, :], Y[0:64, bass.ds(l, 1), :, cols(t)]
                                    .rearrange("p a b c -> p (a b) c")).then_inc(h1_low.sem, 1)
                if name == "proj_v":
                    b = n
                    dve.wait_ge(v_ready.sem, v_ready.at(g - 1, b + 1))
                    dve.wait_ge(o.sem, o.at(g - 1, NQ * (b + 1)))
                    dve.tensor_copy(Voff[0:WIN, b, :], Vcur[WIN:P, b, :]).then_inc(vshift.sem, 1)
                    dve.wait_ge(kt.sem, kt.at(g - 1, b + 1))
                    dve.wait_ge(scores.sem, scores.at(g - 1, NQ * (b + 1)))
                    dve.tensor_copy(KT[:, b, :, 0:WIN], KT[:, b, :, P:WK]).then_inc(kshift.sem, 1)
                if name == "norms":
                    b = n
                    dve.wait_ge(raw.sem, raw.at(g, 2 * b + 2))
                    dve.wait_ge(clamped.sem, clamped.at(g, b))
                    dve.reduce_sum(SS[:, :], SQ[:, :, :, :].rearrange("p c h e -> p (c h) e"), AX_X)\
                       .then_inc(sumsq.sem, 1)
                    tab = lambda k: rope[:, k, bass.ds(t, 1), :, :].rearrange("p a c e -> p (a c) e")
                    spread = lambda a: a.unsqueeze(2).broadcast_to([P, 2, NH, a.shape[-1]])
                    dve.wait_ge(qk.sem, qk.at(g, b - 1))
                    dve.tensor_tensor(T1[:, b % 2, :, :, :], RAW[:, b % 2, :, :, :], spread(tab(0)), ALU.mult)
                    dve.wait_ge(sumsq.sem, sumsq.at(g, b + 1))
                    dve.wait_ge(rnorm.sem, rnorm.at(g, b - 1))
                    dve.tensor_scalar(SC[:, b % 2, :], SS[:, :], 1e-24, None, ALU.max).then_inc(clamped.sem, 1)
                    for h in range(2):
                        a, c = slice(32 * h, 32 * h + 32), slice(32 - 32 * h, 64 - 32 * h)
                        last = dve.tensor_tensor(T2[:, b % 2, :, :, a], RAW[:, b % 2, :, :, c],
                                                 spread(tab(1)[:, :, a]), ALU.mult)
                    last.then_inc(roped.sem, 1)
                if name == "rotate":
                    b = n
                    dve.wait_ge(rope_sum.sem, rope_sum.at(g, b + 1))
                    dve.wait_ge(rnorm.sem, rnorm.at(g, b + 1))
                    dve.wait_ge(qk_turned.sem, qk_turned.at(g, 2 * b))
                    dve.tensor_tensor(QK[:, :, :, :].rearrange("p c q (e k) -> p (c q e) k", k=DH),
                                      T1[:, b % 2, :, :, :].rearrange("p c h k -> p (c h) k"),
                                      RN[:, b % 2, :].unsqueeze(2).broadcast_to([P, 2 * NH, DH]), ALU.mult)\
                       .then_inc(qk.sem, 1)
                if name in ("turn", "turn_alone"):
                    b = n
                    dve.wait_ge(qk_turned.sem, qk_turned.at(g, 2 * b + 2))
                    dve.wait_ge(kshift.sem, kshift.at(g, b + 1))
                    dve.tensor_copy(KT[:, b, :, WIN:WK], proj_bank("kt", b)[:, :].rearrange("p (q c) -> p q c", q=NPAIR))\
                       .then_inc(kt.sem, 1)

            def quad(n, g, t, now, before):
                if now:
                    s = n
                    dve.wait_ge(scores.sem, scores.at(g, s + 1))
                    dve.tensor_reduce(NM[:, s % PR, :], score_ps[s % 2][:, :].rearrange("p (i k) -> p i k", i=QUAD),
                                      AX_X, ALU.max, negate=True).then_inc(negmax.sem, 1)
                s = n - 1
                if now if s >= 0 else before:
                    dve.wait_ge(probs.sem, probs.at(g, s + 1))
                    dve.reciprocal(RDEN[:, s % PR, :], DEN[:, s % PR, :]).then_inc(rden.sem, 1)
                s = n - (LAG - 1)
                if now if s >= 0 else before:
                    dve.wait_ge(p_turned.sem, p_turned.at(g, s + 1))
                    dve.tensor_copy(PT[:, s % 2, :, :].rearrange("p i k -> p (i k)"), turn_ps[s % 2][:, :])\
                       .then_inc(pt.sem, 1)

            def mlp(n, g, t, l):
                if n == 0:
                    dve.wait_ge(mlp_mm.sem, mlp_mm.at(g, 1))
                    dve.tensor_tensor(U[:, :, cols(t)], mlp_ps[0][:, :].rearrange("p (b c) -> p b c", b=NB),
                                      Y[:, bass.ds(l, 1), :, cols(t)].rearrange("p a b c -> p (a b) c"), ALU.add)\
                       .then_inc(u.sem, 1)
                if n == 1:
                    dve.wait_ge(mlp_mm.sem, mlp_mm.at(g, 2))
                    dve.tensor_copy(HC2[:, :], mlp_ps[1][:, :]).then_inc(centred.sem, 1)
                if n == 2:
                    dve.wait_ge(centred.sem, centred.at(g, 1))
                    dve.wait_ge(rstd.sem, rstd.at(g, 1))
                    dve.wait_ge(s_mlp_w, (l + 1) * (16 * N_MLP_LOADS))
                    dve.tensor_tensor(HN[:, :], HC2[:, :], RS[:, :], ALU.mult).then_inc(hn.sem, 1)
                    dve.wait_ge(hn.sem, hn.at(g, 1))
                    dve.tensor_scalar(HN[:, :], HN[:, :], COLS[:, 0:1], COLS[:, 1:2], ALU.mult, ALU.add)\
                       .then_inc(hn.sem, 1)
                if n in (3, 4):
                    for j in range(0, 1) if n == 3 else range(1, NHC):
                        dve.wait_ge(mlp_mm.sem, mlp_mm.at(g, 5 + 2 * j))
                        dve.tensor_scalar(AG[:, 1, j, :], mlp_ps[0][0:HC, :], B1[:, 1, j:j + 1], None, ALU.add)\
                           .then_inc(gate.sem, 1)
                if n == 4:
                    dve.wait_ge(value.sem, value.at(g, NHC))
                    for j in range(NHC):
                        dve.wait_ge(gelu.sem, gelu.at(g, j + 1))
                        dve.tensor_tensor(AG[:, 0, j, :], AG[:, 0, j, :], AG[:, 1, j, :], ALU.mult)\
                           .then_inc(hid.sem, 1)
                if n == 5:
                    other = l * -1 + 1
                    dve.wait_ge(mlp_mm.sem, mlp_mm.at(g, MLP_MM))
                    dve.scalar_tensor_tensor(
                        out=Y[:, bass.ds(other, 1), :, cols(t)].rearrange("p a b c -> p (a b) c"),
                        in0=mlp_ps[1][:, :].rearrange("p (b c) -> p b c", b=NB), scalar=COLS[:, 2:3],
                        in1=U[:, :, cols(t)], op0=ALU.add, op1=ALU.add).then_inc(ynext.sem, 1)

            later = {(2, 1) if part == 2 else at: part for at, part in MLP_AT.items()}
            groups(dve, enter, attention, quad, mlp, later)
            dve.wait_ge(ynext.sem, ynext.at(DEPTH * NT - 1, 1))
            for b in range(NB):
                dve.tensor_tensor(X[:, b * T:(b + 1) * T], X[:, b * T:(b + 1) * T], Y[:, 0, b, PAD:PAD + T], ALU.add)\
                   .then_inc(s_added, 1)
            dve.wait_ge(s_added, NB)

        @block.gpsimd
        def _(pool):
            pool.memset(QT[:, :, :, :, :], 0.0).then_inc(s_zero, 1)
            pool.memset(KT[:, :, :, :], 0.0).then_inc(s_zero, 1)
            pool.memset(Vcur[:, :, :], 0.0).then_inc(s_zero, 1)
            pool.memset(Voff[:, :, :], 0.0).then_inc(s_zero, 1)
            pool.memset(mhalf[:, :], -0.5).then_inc(s_half, 1)
            pool.wait_ge(s_half, 1)
            pool.sem_inc(rnorm.sem, rnorm.credit)
            pool.sem_inc(rope_sum.sem, rope_sum.credit)

            def attention(name, n, g, t, l):
                if name == "norms":
                    b = n
                    pool.wait_ge(clamped.sem, clamped.at(g, b + 1))
                    pool.tensor_tensor(RN[:, b % 2, :], SC[:, b % 2, :], mhalf[:, :], ALU.pow).then_inc(rnorm.sem, 1)
                if name == "sum":
                    b = n
                    pool.wait_ge(roped.sem, roped.at(g, b + 1))
                    pool.tensor_tensor(T1[:, b % 2, :, :, :], T1[:, b % 2, :, :, :], T2[:, b % 2, :, :, :], ALU.add)\
                        .then_inc(rope_sum.sem, 1)

            def quad(n, g, t, now, before):
                s = n - 1
                if now if s >= 0 else before:
                    pool.wait_ge(rden.sem, rden.at(g, s + 1))
                    pool.tensor_tensor(PB[:, s % PR, :, :], PB[:, s % PR, :, :],
                                       RDEN[:, s % PR, :].unsqueeze(2).broadcast_to([P, QUAD, P]), ALU.mult)\
                        .then_inc(normed.sem, 1)

            groups(pool, lambda l: None, attention, quad, None)


def attn_a_stage(nc, d, keep):
    X, ident = keep["X"], keep["ident"]
    with nc.cleanup_on_exit(), ExitStack() as ctx:
        sb, ps, sem = allocators(nc, ctx, "attn_a_")
        XIN = sb("XIN", [P, NB * NT, P])
        XN = sb("XN", [P, NB, PAD + T])
        Wq, Wv, Wg = sb("Wq", [P, CT, P]), sb("Wv", [P, CT, P]), sb("Wg", [P, CT, P])
        Wo = sb("Wo", [P, CT, P])
        heads16 = sb("heads16", [P, P])
        cw, cb = sb("cw", [P, 4]), sb("cb", [P, 1])
        gb, lg, lb = sb("gb", [P, CT]), sb("lg", [P, 1]), sb("lb", [P, 1])
        freqs, gamma = sb("freqs", [P, CT]), sb("gamma", [P, CT])
        pos = sb("pos", [P, T])
        turns = sb("turns", [P, T])
        ang = sb("ang", [P, T])
        cos = sb("cos", [P, CT, T])
        decay = sb("decay", [P, CT, T])
        rdecay = sb("rdecay", [P, CT, T])
        gpow = sb("gpow", [P, 11, CT])
        ones = sb("ones", [P, T])
        shift = sb("shift", [P, 1])
        XC = sb("XC", [P, T])
        SQ = sb("SQ", [P, T])
        RAW = sb("RAW", [P, T])
        RN = sb("RN", [P, T])
        Q = sb("Q", [P, PAD + T])
        A = sb("A", [P, T])
        G = sb("G", [P, T])
        M = sb("M", [P, T])
        OUT = sb("OUT", [P, CT, T])
        RS = sb("RS", [P, NB, T])
        bank = [ps(f"bank{i}", [P, 512]) for i in range(8)]
        norm = Norm(sem, keep, NB * T // 512, bank[0:4], dst=half_columns(XN, PAD),
                    rs=lambda c: XIN[:, 4 * c:4 * c + 4, :].rearrange("p t c -> p (t c)"),
                    sq=SQ[:, :].rearrange("p (a t) -> p a t", a=2))
        O = XIN
        end = Norm(lambda name: sem("end_" + name), keep, NB * T // 512, bank[0:4], dst=half_columns(XN, PAD),
                   rs=half_columns(RS), sq=SQ[:, :].rearrange("p (a t) -> p a t", a=2))
        qk_ps, ss_ps, v_ps, g_ps = (bank[2 * i:2 * i + 2] for i in range(4))

        s_x, s_w, s_xt, s_xe, s_zero, s_tab, s_gp, s_trig, s_sin, s_gamma, s_angle = (
            sem(n) for n in ("x", "w", "xt", "xe", "zero", "tab", "gp", "trig", "sin", "gamma", "angle"))
        count = lambda name, per, credit=0: Count(sem(name), per, credit)
        qk_mm, ss_mm, v_mm, g_mm = (count(n, 1, 1) for n in ("qk_mm", "ss_mm", "v_mm", "g_mm"))
        squared, copied, clamped, lnq, rnorm, gated = (
            count(n, 1, 1) for n in ("squared", "copied", "clamped", "lnq", "rnorm", "gated"))
        q_ready, kcos, decayed, av, avg, summed, scaled, out_ready = (
            count(n, 1, 1) for n in ("q_ready", "kcos", "decayed", "av", "avg", "summed", "scaled", "out_ready"))
        conv = count("conv", 4)
        o_mm, o_read = count("o_mm", 1, 1), count("o_read", 1, 1)
        s_gained, s_added = sem("gained"), sem("added")
        NWA = 13

        block = ctx.enter_context(nc.Block())

        @block.sync
        def _(sp):
            sp.dma_start(gamma[:, :], d["gamma"]).then_inc(s_gamma, 16)
            for b in range(NB):
                sp.dma_start(XIN[:, b * NT:(b + 1) * NT, :], d["x"][b].rearrange("(t p) c -> p t c", p=P)).then_inc(s_x, 16)
            for n in ("ident", "centre", "mean", "eps", "identb"):
                sp.dma_start(keep[n][:, :], d[n]).then_inc(s_x, 16)

        @block.gpsimd
        def _(pool):
            for dst, src in ((pos[:, :], d["pos"].broadcast_to([P, T])), (freqs[:, :], d["freqs"]),
                             (cw[:, :], d["conv_w"]), (cb[:, :], d["conv_b"]),
                             (Wq[:, :, :], d["qk_wT"].rearrange("k (c n) -> k c n", c=CT)),
                             (heads16[:, :], d["heads16"]),
                             (Wv[:, :, :], d["v_wT"].rearrange("k (c n) -> k c n", c=CT)),
                             (Wg[:, :, :], d["g_wT"].rearrange("k (c n) -> k c n", c=CT)),
                             (Wo[:, :, :], d["o_wT"].rearrange("(c k) n -> k c n", c=CT)),
                             (gb[:, :], d["g_b"]), (lg[:, :], d["ln_g"]), (lb[:, :], d["ln_b"]),
                             (shift[:, :], d["shift"])):
                pool.dma_start(dst, src).then_inc(s_w, 16)
            pool.wait_ge(s_w, 16 * NWA)
            pool.sem_inc(decayed.sem, decayed.credit)
            pool.wait_ge(s_tab, TABLES)
            pool.wait_ge(s_sin, CT)
            with pool.Fori(0, NB) as b:
                for c in range(CT):
                    n = b * CT + c
                    pool.wait_ge(gated.sem, gated.at(n, 1))
                    pool.tensor_tensor(G[:, :], G[:, :], decay[:, c, :], ALU.mult).then_inc(decayed.sem, 1)

        @block.tensor
        def _(pe):
            pe.wait_ge(s_x, 16 * 9)
            for c in range(NB * T // 512):
                if c >= 2:
                    pe.wait_ge(s_xe, c - 1)
                for i in range(4):
                    last = pe.transpose(bank[4 + c % 2][:, i * P:(i + 1) * P], XIN[:, 4 * c + i, :], ident[:, :])
                last.then_inc(s_xt, 1)
            norm.tensor(pe, lambda c: X[:, c * 512:(c + 1) * 512], lambda pe, c: pe.wait_ge(s_xe, c + 1))
            for c in (qk_mm, ss_mm, v_mm, g_mm, o_mm):
                pe.sem_inc(c.sem, c.credit)
            pe.wait_ge(s_w, 16 * NWA)
            pe.wait_ge(norm.s_out, norm.chunks)

            def product(banks, weights, source):
                for h in range(2):
                    last = pe.matmul(banks[h][:, :], weights, source[:, h * 512:(h + 1) * 512], start=True, stop=True)
                return last

            with pe.Fori(0, NB) as b:
                pe.wait_ge(conv.sem, conv.at(b, 4))
                for c in range(CT):
                    n = b * CT + c
                    if c == 0:
                        pe.wait_ge(o_read.sem, o_read.at(b, 0))
                    pe.wait_ge(copied.sem, copied.at(n, 0))
                    product(qk_ps, Wq[:, c, :], XC).then_inc(qk_mm.sem, 1)
                    pe.wait_ge(gated.sem, gated.at(n, 0))
                    product(g_ps, Wg[:, c, :], XC).then_inc(g_mm.sem, 1)
                    pe.wait_ge(squared.sem, squared.at(n, 1))
                    pe.wait_ge(clamped.sem, clamped.at(n, 0))
                    product(ss_ps, heads16[:, :], SQ).then_inc(ss_mm.sem, 1)
                    pe.wait_ge(av.sem, av.at(n, 0))
                    product(v_ps, Wv[:, c, :], XC).then_inc(v_mm.sem, 1)
                pe.wait_ge(out_ready.sem, out_ready.at(b * CT, CT))
                pe.wait_ge(copied.sem, copied.at(b * CT, CT))
                for h in range(2):
                    for c in range(CT):
                        last = pe.matmul(qk_ps[h][:, :], Wo[:, c, :], OUT[:, c, h * 512:(h + 1) * 512],
                                         start=(c == 0), stop=(c == CT - 1))
                last.then_inc(o_mm.sem, 1)
            pe.wait_ge(o_read.sem, o_read.at(NB - 1, 1))
            pe.wait_ge(clamped.sem, clamped.at(NB * CT, 0))
            end.tensor(pe, lambda c: O[:, 4 * c:4 * c + 4, :].rearrange("p t c -> p (t c)"))

        @block.scalar
        def _(act):
            for c in range(NB * T // 512):
                act.wait_ge(s_xt, c + 1)
                act.activation(X[:, c * 512:(c + 1) * 512], bank[4 + c % 2][:, :], ACT.Copy).then_inc(s_xe, 1)
            norm.scalar(act)
            for c in range(CT):
                act.wait_ge(s_trig, 6 * c + 6)
                act.activation(cos[:, c, :], cos[:, c, :], ACT.Sin).then_inc(s_sin, 1)
            for c in (squared, copied, lnq, rnorm, gated):
                act.sem_inc(c.sem, c.credit)
            act.wait_ge(s_w, 16 * NWA)

            def halves(dst, banks, func, **more):
                for h in range(2):
                    last = act.activation(dst[:, h * 512:(h + 1) * 512], banks[h][:, :], func, **more)
                return last

            with act.Fori(0, NB) as b:
                for c in range(CT):
                    n = b * CT + c
                    act.wait_ge(qk_mm.sem, qk_mm.at(n, 1))
                    act.wait_ge(ss_mm.sem, ss_mm.at(n, 0))
                    halves(SQ, qk_ps, ACT.Square).then_inc(squared.sem, 1)
                    act.wait_ge(q_ready.sem, q_ready.at(n, 0))
                    halves(RAW, qk_ps, ACT.Copy).then_inc(copied.sem, 1)
                    act.wait_ge(clamped.sem, clamped.at(n, 1))
                    act.activation(RN[:, :], RN[:, :], ACT.Ln, scale=float(2 ** 20)).then_inc(lnq.sem, 1)
                    act.wait_ge(lnq.sem, lnq.at(n, 1))
                    act.activation(RN[:, :], RN[:, :], ACT.Exp, scale=-0.5, bias=shift[:, :]).then_inc(rnorm.sem, 1)
                    act.wait_ge(g_mm.sem, g_mm.at(n, 1))
                    act.wait_ge(avg.sem, avg.at(n, 0))
                    halves(G, g_ps, ACT.Sigmoid, bias=gb[:, c:c + 1]).then_inc(gated.sem, 1)
            end.scalar(act)

        @block.vector
        def _(dve):
            dve.memset(XN[:, :, 0:PAD], 0.0)
            dve.memset(Q[:, 0:PAD], 0.0)
            dve.memset(ones[:, :], 1.0).then_inc(s_zero, 1)

            dve.wait_ge(s_gamma, 16)
            dve.tensor_copy(gpow[:, 0, :], gamma[:, :]).then_inc(s_gp, 1)
            for i in range(10):
                dve.wait_ge(s_gp, i + 1)
                dve.tensor_tensor(gpow[:, i + 1, :], gpow[:, i, :], gpow[:, i, :], ALU.mult).then_inc(s_gp, 1)
            dve.memset(decay[:, :, 0:1], 1.0).then_inc(s_tab, 1)
            at = 1
            for i in range(10):
                n = 1 << i
                for c in range(CT):
                    dve.wait_ge(s_tab, at - c)
                    dve.tensor_scalar(decay[:, c, n:2 * n], decay[:, c, 0:n], gpow[:, i, c:c + 1], None, ALU.mult)\
                       .then_inc(s_tab, 1)
                    at += 1
            dve.wait_ge(s_tab, at)
            dve.tensor_scalar(rdecay[:, :, :], decay[:, :, :], 1e-6, None, ALU.add).then_inc(s_tab, 1)
            dve.wait_ge(s_tab, at + 1)
            dve.reciprocal(rdecay[:, :, :], rdecay[:, :, :]).then_inc(s_tab, 1)
            dve.wait_ge(s_tab, at + 2)
            assert at + 2 == TABLES
            norm.vector(dve)
            dve.wait_ge(s_w, 16 * NWA)
            TURN1 = 201 / 32
            TURN2 = 507 * 2.0 ** -18
            TURN3 = 2 * math.pi - TURN1 - TURN2
            BIG = 1.5 * 2.0 ** 23
            k = 0
            for c in range(CT):
                ang_c = cos[:, c, :]

                def done(ins):
                    nonlocal k
                    k += 1
                    ins.then_inc(s_trig, 1)
                    dve.wait_ge(s_trig, k)

                dve.tensor_scalar(ang_c, pos[:, :], freqs[:, c:c + 1], None, ALU.mult).then_inc(s_angle, 1)
                dve.wait_ge(s_angle, c + 1)
                done(dve.tensor_scalar(turns[:, :], ang_c, 1 / (2 * math.pi), 0.25, ALU.mult, ALU.add))
                done(dve.tensor_scalar(turns[:, :], turns[:, :], BIG, None, ALU.add))
                done(dve.tensor_scalar(turns[:, :], turns[:, :], -BIG, None, ALU.add))
                dve.scalar_tensor_tensor(out=ang[:, :], in0=turns[:, :], scalar=-TURN1, in1=ang_c,
                                         op0=ALU.mult, op1=ALU.add).then_inc(s_zero, 1)
                dve.wait_ge(s_zero, 2 + 2 * c)
                dve.scalar_tensor_tensor(out=ang[:, :], in0=turns[:, :], scalar=-TURN2, in1=ang[:, :],
                                         op0=ALU.mult, op1=ALU.add).then_inc(s_zero, 1)
                dve.wait_ge(s_zero, 3 + 2 * c)
                done(dve.scalar_tensor_tensor(out=ang[:, :], in0=turns[:, :], scalar=-TURN3, in1=ang[:, :],
                                              op0=ALU.mult, op1=ALU.add))
                done(dve.tensor_scalar(ang[:, :], ang[:, :], math.pi / 2, 3.1415925, ALU.add, ALU.min))
                done(dve.tensor_scalar(ang_c, ang[:, :], -3.1415925, None, ALU.max))
            for c in (clamped, q_ready, kcos, av, avg, summed, scaled, out_ready, o_read):
                dve.sem_inc(c.sem, c.credit)
            dve.wait_ge(norm.s_out, norm.chunks)

            with dve.Fori(0, NB) as b:
                tap = lambda j: XN[:, bass.ds(b, 1), PAD - 3 + j:PAD - 3 + j + T].rearrange("p a t -> p (a t)")
                dve.wait_ge(g_mm.sem, g_mm.at(b * CT, 0))
                dve.wait_ge(v_mm.sem, v_mm.at(b * CT, 0))
                dve.tensor_scalar(XC[:, :], tap(3), cw[:, 3:4], cb[:, :], ALU.mult, ALU.add).then_inc(conv.sem, 1)
                for j in range(3):
                    dve.wait_ge(conv.sem, conv.at(b, j + 1))
                    dve.scalar_tensor_tensor(out=XC[:, :], in0=tap(j), scalar=cw[:, j:j + 1], in1=XC[:, :],
                                             op0=ALU.mult, op1=ALU.add).then_inc(conv.sem, 1)

                def clamp(n):
                    dve.wait_ge(ss_mm.sem, ss_mm.at(n, 1))
                    for h in range(2):
                        last = dve.tensor_scalar(RN[:, h * 512:(h + 1) * 512], ss_ps[h][:, :], 1e-24, None, ALU.max)
                    last.then_inc(clamped.sem, 1)

                clamp(b * CT)
                for c in range(CT):
                    n = b * CT + c
                    dve.wait_ge(rnorm.sem, rnorm.at(n, 1))
                    dve.wait_ge(copied.sem, copied.at(n, 1))
                    dve.wait_ge(out_ready.sem, out_ready.at(n, 0))
                    dve.tensor_tensor(Q[:, PAD:PAD + T], RAW[:, :], RN[:, :], ALU.mult).then_inc(q_ready.sem, 1)
                    dve.wait_ge(q_ready.sem, q_ready.at(n, 1))
                    dve.wait_ge(summed.sem, summed.at(n, 0))
                    dve.tensor_tensor(A[:, :], cos[:, c, :], Q[:, PAD - 1:PAD - 1 + T], ALU.add)\
                       .then_inc(kcos.sem, 1)
                    if c + 1 < CT:
                        clamp(n + 1)
                    dve.wait_ge(kcos.sem, kcos.at(n, 1))
                    dve.wait_ge(v_mm.sem, v_mm.at(n, 1))
                    for h in range(2):
                        a = A[:, h * 512:(h + 1) * 512]
                        last = dve.tensor_tensor(a, v_ps[h][:, :], a, ALU.mult)
                    last.then_inc(av.sem, 1)
                    dve.wait_ge(av.sem, av.at(n, 1))
                    dve.wait_ge(decayed.sem, decayed.at(n, 1))
                    dve.tensor_tensor(A[:, :], A[:, :], G[:, :], ALU.mult).then_inc(avg.sem, 1)
                    dve.wait_ge(avg.sem, avg.at(n, 1))
                    dve.tensor_tensor_scan(M[:, :], ones[:, :], A[:, :], 0.0, ALU.mult, ALU.add)\
                       .then_inc(summed.sem, 1)
                    dve.wait_ge(summed.sem, summed.at(n, 1))
                    dve.tensor_tensor(M[:, :], M[:, :], rdecay[:, c, :], ALU.mult).then_inc(scaled.sem, 1)
                    dve.wait_ge(scaled.sem, scaled.at(n, 1))
                    dve.wait_ge(q_ready.sem, q_ready.at(n, 1))
                    if c == 0:
                        dve.wait_ge(o_mm.sem, o_mm.at(b, 0))
                    dve.tensor_tensor(OUT[:, c, :], M[:, :], Q[:, PAD:PAD + T], ALU.mult).then_inc(out_ready.sem, 1)
                dve.wait_ge(o_mm.sem, o_mm.at(b, 1))
                for h in range(2):
                    last = dve.tensor_copy(O[:, bass.ds(b * NT + 4 * h, 4), :].rearrange("p t c -> p (t c)"),
                                           qk_ps[h][:, :])
                last.then_inc(o_read.sem, 1)
            end.vector(dve)
            for c in range(end.chunks):
                dve.wait_ge(end.s_out, c + 1)
                x = X[:, c * 512:(c + 1) * 512]
                dve.scalar_tensor_tensor(out=x, in0=end.dst(c), scalar=lg[:, 0:1], in1=x,
                                         op0=ALU.mult, op1=ALU.add).then_inc(s_gained, 1)
                dve.wait_ge(s_gained, c + 1)
                dve.tensor_scalar(x, x, lb[:, :], None, ALU.add).then_inc(s_added, 1)
            dve.wait_ge(s_added, end.chunks)


def wait(eng, sem, value):
    if not isinstance(value, int) or value > 0:
        eng.wait_ge(sem, value)


def attn_b_stage(nc, d, keep):
    X = keep["X"]
    with nc.cleanup_on_exit(), ExitStack() as ctx:
        sb, ps, sem = allocators(nc, ctx, "attn_b_")
        XN = sb("XN", [P, NB, T])
        XB = sb("XB", [P, T])
        W = sb("W", [P, 4, P])
        Wv, Wo = sb("Wv", [P, P]), sb("Wo", [P, P])
        rope = sb("rope", [P, 4, T])
        causal = sb("causal", [P, 2, P], BF16)
        T1, T2 = sb("T1", [P, T]), sb("T2", [P, T])
        R = sb("R", [P, T])
        RP = sb("RP", [P, 2, PARTS, T], BF16)
        VB = sb("VB", [P, NG, NT, BG, BD + 1])
        VQ = sb("VQ", [P, BG, NT, BD + 1])
        QS = sb("QS", [KS9 + PARTS, BG, T], BF16)
        KS = sb("KS", [KS9 + PARTS, BG, T], BF16)
        ones = sb("ones", [PARTS, BG, T], BF16)
        NX = sb("NX", [P, 2, 2, NT])
        NM = sb("NM", [P, 2, NT])
        NP = sb("NP", [P, 2, PARTS, NT], BF16)
        NR = sb("NR", [P, 2, NT])
        zeros = sb("zeros", [P, NT])
        MT = sb("MT", [PARTS * NT, 2, P], BF16)
        PT = sb("PT", [P, 4, T])
        OS = sb("OS", [BD + 1, 2, T])
        OA = sb("OA", [P, 2, T])
        DA = sb("DA", [P, 2, T])
        DEN = sb("DEN", [P, NB * BH * T // P])
        s1_ps = [ps(f"s1_{i}", [P, 512]) for i in range(2)]
        o_ps = [ps(f"o_{i}", [P, 512]) for i in range(2)]
        s2_ps = [ps(f"s2_{i}", [P, 1024]) for i in range(2)]
        qk_dram = nc.dram_tensor("attn_b_qk_parts", (2, PARTS, NB * P, T), BF16, kind="Internal").ap()
        o_dram = nc.dram_tensor("attn_b_o", (NB * BH, BD + 1, T), F32, kind="Internal").ap()
        rden_dram = nc.dram_tensor("attn_b_rden", (P, NB * BH * T // P), F32, kind="Internal").ap()
        norm = Norm(sem, keep, NB * T // 512, [o_ps[0], o_ps[1], s1_ps[0], s1_ps[1]], dst=half_columns(XN),
                    rs=half_columns(PT), sq=T1[:, :].rearrange("p (a t) -> p a t", a=2))

        s_w, s_set, s_zeros = sem("w"), sem("set"), sem("zeros")
        count = lambda name, per: Count(sem(name), per)
        xb, ab_mm, v_mm = count("xb", 1), count("ab_mm", 4), count("v_mm", 1)
        turned, rsum, p1, r1, p2, p3 = (count("rotated", 4), count("rsum", 2), count("p1", 2), count("r1", 2),
                                        count("p2", 2), count("p3", 2))
        s_parts_out = [sem("q_out"), sem("k_out")]
        v_copied = count("v_copied", 1)
        UNITS = 13
        TURN = 3
        s_load = [sem(f"load{h}") for h in range(BG)]
        s_rows = [sem(f"rows{h}") for h in range(BG)]
        s_stored = [sem(f"stored{i}") for i in range(2)]
        s1_mm, s1_read = count("s1_mm", UNITS * BG), count("s1_read", UNITS * BG)
        parts = count("parts", 4 * BG)
        maxima = count("maxima", BG)
        s2_mm, probs, pv = count("s2_mm", NT * BG), count("probs", NT * BG), count("pv", NT * BG)
        vq, o_read = count("vq", BG), count("o_read", 2 * BG)
        s_back = [sem("back0"), sem("back1")]
        s_den = sem("den")
        s_rden, s_scaled, s_out_mm, s_added = sem("rden"), sem("scaled"), sem("out_mm"), sem("added")

        CHUNKS = [(i, c) for i in reversed(range(NT)) for c in range(i // 4 + 1)]
        SLOTS = [1, 1, 1, 1, 1, 1, 2, 2, 2, 1]
        assert len(CHUNKS) == UNITS - 1 and sum(SLOTS) == UNITS

        def over_groups(eng, step, last=NG):
            for h in range(BG):
                step(0, h, True, h >= 1, h >= 2)
            with eng.Fori(1, last) as n:
                for h in range(BG):
                    step(n, h, True, True, True)

        def over_sequences(eng, work):
            work(0)
            with eng.Fori(1, NB) as b:
                work(b)

        def chunk_keys(i, c):
            return c * 512, min((c + 1) * 512, (i + 1) * P)

        block = ctx.enter_context(nc.Block())

        @block.sync
        def _(sp):
            for i, n in enumerate(("WqT", "WqpT", "WkT", "WkpT")):
                sp.dma_start(W[:, i, :], d[n]).then_inc(s_w, 16)
            sp.dma_start(Wv[:, :], d["WvT"]).then_inc(s_w, 16)
            sp.dma_start(rope[:, :, :], d["rope"]).then_inc(s_w, 16)
            sp.dma_start(causal[:, :, :], d["causal"]).then_inc(s_w, 16)
            sp.dma_start(Wo[:, :], d["WoT"]).then_inc(s_w, 16)
            sp.wait_ge(s_set, 1)
            sp.dma_start(KS[KS9:KS9 + PARTS, :, :], ones[:, :, :]).then_inc(s_w, 16)

            def store_parts(b):
                for w in range(2):
                    sp.wait_ge(p3.sem, p3.at(b, w + 1))
                    sp.dma_start(qk_dram[w][:, bass.ds(b * P, P), :].rearrange("a c t -> c a t"), RP[:, w, :, :])\
                      .then_inc(s_parts_out[w], 16)

            over_sequences(sp, store_parts)
            for w in range(2):
                sp.wait_ge(s_parts_out[w], 16 * NB)

            def load(n, h):
                rows = bass.ds(n * (BG * BD) + h * BD, BD)
                for a in range(PARTS):
                    at = slice(a * PARTS * BD, (a + 1) * PARTS * BD)
                    q = qk_dram[0][a, rows, :].unsqueeze(0).broadcast_to([PARTS, BD, T])
                    k = qk_dram[1][:, rows, :]
                    sp.dma_start(QS[at, h, :], q).then_inc(s_load[h], 16)
                    sp.dma_start(KS[at, h, :], k).then_inc(s_load[h], 16)

            for h in range(BG):
                load(0, h)

            def step(n, h, s1, turn, s2, ahead=True):
                k = (h - 1) % BG
                if turn:
                    sp.wait_ge(s1_read.sem, s1_read.at(n, UNITS * h + TURN + 1))
                    sp.dma_start(QS[KS9:KS9 + PARTS, k, :], MT[:, k % 2, :]).then_inc(s_rows[k], 16)
                if s2:
                    k = (h - 2) % BG
                    if ahead:
                        sp.wait_ge(s2_mm.sem, s2_mm.at(n, NT * (h - 1)))
                        load(n + (h - 2 - k) // BG + 1, k)
                    sp.wait_ge(o_read.sem, o_read.at(n, 2 * (h - 1)))
                    sp.dma_start(o_dram[bass.ds(n * BG + h - 2, 1), :, :].rearrange("a e t -> (a e) t"),
                                 OS[:, h % 2, :]).then_inc(s_stored[h % 2], 16)

            over_groups(sp, step, NG - 1)
            for h in range(BG):
                step(NG - 1, h, True, True, True, ahead=h < 2)
            step(NG, 0, False, True, True, ahead=False)
            step(NG, 1, False, False, True, ahead=False)
            for i in range(2):
                sp.wait_ge(s_stored[i], 16 * NG * BG // 2)
            spread = lambda a: a.rearrange("a e (k t) -> a (e k) t", k=2)
            sp.dma_start(DEN[:, :], spread(o_dram[:, BD:BD + 1, :])).then_inc(s_den, 16)
            for b in range(2):
                sp.dma_start(OA[:, b, :], o_dram[b * BH:(b + 1) * BH, 0:BD, :]).then_inc(s_back[b], 16)
            sp.wait_ge(s_rden, 1)
            sp.dma_start(rden_dram, DEN[:, :]).then_inc(s_den, 16)
            sp.wait_ge(s_den, 32)
            for b in range(NB):
                if b >= 2:
                    sp.wait_ge(s_out_mm, b - 1)
                    sp.dma_start(OA[:, b % 2, :], o_dram[b * BH:(b + 1) * BH, 0:BD, :]).then_inc(s_back[b % 2], 16)
                rows = rden_dram[2 * b * BH:2 * (b + 1) * BH, :].rearrange("(a k) t -> a (k t)", k=2)
                sp.dma_start(DA[:, b % 2, :], rows.unsqueeze(1).broadcast_to([BH, BD, T])).then_inc(s_back[b % 2], 16)

        @block.tensor
        def _(pe):
            norm.tensor(pe, lambda c: X[:, c * 512:(c + 1) * 512])
            pe.wait_ge(s_w, 16 * 9)
            pe.wait_ge(norm.s_out, norm.chunks)

            def project(b):
                pe.wait_ge(xb.sem, xb.at(b, 1))
                for w in range(4):
                    wait(pe, turned.sem, turned.at(b, w - 1))
                    for h in range(2):
                        last = pe.matmul(s2_ps[w % 2][:, h * 512:(h + 1) * 512], W[:, w, :],
                                         XB[:, h * 512:(h + 1) * 512], start=True, stop=True)
                    last.then_inc(ab_mm.sem, 1)
                wait(pe, v_copied.sem, v_copied.at(b, 0))
                for t in range(NT):
                    last = pe.matmul(s1_ps[t // 4][:, t % 4 * P:(t % 4 + 1) * P], XB[:, t * P:(t + 1) * P], Wv[:, :],
                                     start=True, stop=True)
                last.then_inc(v_mm.sem, 1)

            over_sequences(pe, project)
            pe.wait_ge(v_copied.sem, NB)
            pe.wait_ge(turned.sem, 4 * NB)

            def max_unit(n, h, u):
                i, c = CHUNKS[u if u < TURN else u - 1]
                lo, hi = chunk_keys(i, c)
                bank = s1_ps[(UNITS * h + u) % 2]
                wait(pe, s1_read.sem, s1_read.at(n, UNITS * h + u - 1))
                diagonal = hi == (i + 1) * P
                if diagonal:
                    pe.matmul(bank[:, hi - lo - P:hi - lo], keep["identb"][:, :], causal[:, 0, :], start=True,
                              stop=True)
                pe.matmul(bank[:, 0:hi - lo], QS[0:KS9, h, i * P:(i + 1) * P], KS[0:KS9, h, lo:hi],
                          start=not diagonal, stop=True, skip_group_check=True).then_inc(s1_mm.sem, 1)

            def turn_unit(n, h):
                bank = s1_ps[(UNITS * h + TURN) % 2]
                k = (h - 1) % BG
                wait(pe, s1_read.sem, s1_read.at(n, UNITS * h + TURN - 1))
                pe.wait_ge(parts.sem, parts.at(n, 4 * h))
                pe.matmul(bank[0:PARTS * NT, 0:P], NP[:, k % 2, :, :].rearrange("p a i -> p (a i)"),
                          keep["identb"][:, :], start=True, stop=True).then_inc(s1_mm.sem, 1)

            def exp_unit(n, h, j):
                k = (h - 2) % BG
                width = T - j * P
                bank = s2_ps[j % 2]
                wait(pe, probs.sem, probs.at(n, NT * (h - 2) + j - 1))
                if j == 0:
                    pe.wait_ge(s_rows[k], 16 * (n + 1 + (h - 2 - k) // BG))
                pe.matmul(bank[:, 0:P], keep["identb"][:, :], causal[:, 1, :], start=True, stop=True)
                for lo in range(0, width, 512):
                    hi = min(width, lo + 512)
                    last = pe.matmul(bank[:, lo:hi], KS[:, k, j * P:(j + 1) * P], QS[:, k, j * P + lo:j * P + hi],
                                     start=lo > 0, stop=True, skip_group_check=True)
                last.then_inc(s2_mm.sem, 1)

            def value_unit(n, h, j):
                k = (h - 2) % BG
                if j == 0:
                    wait(pe, o_read.sem, o_read.at(n, 2 * (h - 2)))
                    pe.wait_ge(vq.sem, vq.at(n, h - 1))
                pe.wait_ge(probs.sem, probs.at(n, NT * (h - 2) + j + 1))
                for half in range(j // 4, 2):
                    lo, hi = max(j * P, half * 512), (half + 1) * 512
                    last = pe.matmul(o_ps[half][0:BD + 1, lo - half * 512:512], VQ[:, k, j, :],
                                     PT[:, j % 4, lo - j * P:hi - j * P], start=(j == 0), stop=(j % 4 == 3),
                                     skip_group_check=True)
                last.then_inc(pv.sem, 1)

            def step(n, h, s1, turn, s2):
                if s1:
                    pe.wait_ge(s_load[h], 96 * (n + 1))
                elif h == 0:
                    pe.wait_ge(s1_read.sem, s1_read.at(n, 0))
                    pe.sem_inc(s1_mm.sem, TURN)
                u = 0
                for slot, units in enumerate(SLOTS):
                    if s2 and slot < NT:
                        exp_unit(n, h, slot)
                    for u in range(u, u + units):
                        if u == TURN:
                            if turn:
                                turn_unit(n, h)
                            elif s1:
                                pe.wait_ge(s1_read.sem, s1_read.at(n, u))
                                pe.sem_inc(s1_mm.sem, 1)
                        elif s1:
                            max_unit(n, h, u)
                    u += 1
                    if s2 and slot >= 2:
                        value_unit(n, h, slot - 2)

            over_groups(pe, step)
            step(NG, 0, False, True, True)
            step(NG, 1, False, False, True)
            for b in range(NB):
                pe.wait_ge(s_scaled, b + 1)
                if b >= 2:
                    pe.wait_ge(s_added, b - 1)
                for h in range(2):
                    last = pe.matmul(s2_ps[b % 2][:, h * 512:(h + 1) * 512], Wo[:, :],
                                     OA[:, b % 2, h * 512:(h + 1) * 512], start=True, stop=True)
                last.then_inc(s_out_mm, 1)

        @block.scalar
        def _(act):
            norm.scalar(act)

            def split(b):
                for w in range(2):
                    act.wait_ge(rsum.sem, rsum.at(b, w + 1))
                    wait(act, s_parts_out[w], 16 * b)
                    act.activation(RP[:, w, 0, :], R[:, :], ACT.Copy).then_inc(p1.sem, 1)
                    act.wait_ge(r1.sem, r1.at(b, w + 1))
                    act.activation(RP[:, w, 1, :], R[:, :], ACT.Copy).then_inc(p2.sem, 1)

            over_sequences(act, split)

            def step(n, h, s1, turn, s2):
                if not s2:
                    return

                def copy_out(half):
                    act.wait_ge(pv.sem, pv.at(n, NT * (h - 2) + 4 * half + 4))
                    if half == 0:
                        wait(act, s_stored[h % 2], 32 * n + 16 * (h // 2 - 1))
                    act.activation(OS[:, h % 2, half * 512:(half + 1) * 512], o_ps[half][0:BD + 1, :], ACT.Copy)\
                       .then_inc(o_read.sem, 1)

                for j in range(NT):
                    width = T - j * P
                    act.wait_ge(s2_mm.sem, s2_mm.at(n, NT * (h - 2) + j + 1))
                    wait(act, pv.sem, pv.at(n, NT * (h - 2) + j - 3))
                    act.activation(PT[:, j % 4, 0:width], s2_ps[j % 2][:, 0:width], ACT.Exp).then_inc(probs.sem, 1)
                    if j == 6:
                        copy_out(0)
                copy_out(1)

            over_groups(act, step)
            step(NG, 0, False, True, True)
            step(NG, 1, False, False, True)

        @block.vector
        def _(dve):
            dve.memset(ones[:, :, :], 1.0).then_inc(s_set, 1)
            dve.memset(NX[:, :, 1, 0:4], 3e38).then_inc(s_set, 1)
            norm.vector(dve)
            dve.wait_ge(s_w, 16 * 9)
            dve.wait_ge(s_set, 2)
            dve.wait_ge(s_zeros, 2)

            def rotate(b):
                for w in range(2):
                    if w == 0:
                        wait(dve, p3.sem, p3.at(b, 0))
                    for i, dst in enumerate((T1, T2)):
                        dve.wait_ge(ab_mm.sem, ab_mm.at(b, 2 * w + i + 1))
                        wait(dve, rsum.sem, rsum.at(b, w))
                        for h in range(2):
                            half = slice(h * 512, (h + 1) * 512)
                            last = dve.tensor_tensor(dst[:, half], s2_ps[i][:, half], rope[:, 2 * w + i, half], ALU.mult)
                        last.then_inc(turned.sem, 1)
                    dve.wait_ge(turned.sem, turned.at(b, 2 * w + 2))
                    wait(dve, p3.sem, p3.at(b, w))
                    dve.tensor_tensor(R[:, :], T1[:, :], T2[:, :], ALU.add).then_inc(rsum.sem, 1)
                    dve.wait_ge(p1.sem, p1.at(b, w + 1))
                    dve.wait_ge(rsum.sem, rsum.at(b, w + 1))
                    dve.tensor_tensor(R[:, :], R[:, :], RP[:, w, 0, :], ALU.subtract).then_inc(r1.sem, 1)
                    dve.wait_ge(p2.sem, p2.at(b, w + 1))
                    dve.wait_ge(r1.sem, r1.at(b, w + 1))
                    dve.tensor_tensor(RP[:, w, 2, :], R[:, :], RP[:, w, 1, :], ALU.subtract).then_inc(p3.sem, 1)
                dve.wait_ge(v_mm.sem, v_mm.at(b, 1))
                for g in range(BH // BG):
                    for half in range(2):
                        v = s1_ps[half][:, :].rearrange("p (t g h e) -> p t g h e", t=4, g=BH // BG, h=BG)[:, :, g]
                        last = dve.tensor_copy(
                            VB[:, bass.ds(b * (BH // BG) + g, 1), 4 * half:4 * half + 4, :, 0:BD]
                            .rearrange("p a t h e -> p (a t) h e"), v)
                last.then_inc(v_copied.sem, 1)

            over_sequences(dve, rotate)
            dve.wait_ge(v_copied.sem, NB)

            def step(n, h, s1, turn, s2):
                if s1:
                    wait(dve, pv.sem, pv.at(n, NT * (h - 3)))
                    dve.tensor_copy(VQ[:, h, :, :], VB[:, bass.ds(n, 1), :, h, :].rearrange("p a t e -> p (a t) e"))\
                       .then_inc(vq.sem, 1)
                    wait(dve, parts.sem, parts.at(n, 4 * (h - 1)))
                elif h == 0:
                    dve.wait_ge(s1_mm.sem, s1_mm.at(n, TURN))
                    dve.sem_inc(s1_read.sem, TURN)
                for u in range(UNITS):
                    bank = s1_ps[(UNITS * h + u) % 2]
                    if u == TURN:
                        if turn:
                            k = (h - 1) % BG
                            dve.wait_ge(s1_mm.sem, s1_mm.at(n, UNITS * h + u + 1))
                            o = (h - 3) % BG
                            wait(dve, s_rows[o], 16 * (n + 1 + (h - 3 - o) // BG))
                            dve.tensor_copy(MT[:, k % 2, :], bank[0:PARTS * NT, 0:P]).then_inc(s1_read.sem, 1)
                        elif s1:
                            dve.wait_ge(s1_mm.sem, s1_mm.at(n, u + 1))
                            dve.sem_inc(s1_read.sem, 1)
                    elif s1:
                        i, c = CHUNKS[u if u < TURN else u - 1]
                        lo, hi = chunk_keys(i, c)
                        dve.wait_ge(s1_mm.sem, s1_mm.at(n, UNITS * h + u + 1))
                        dve.tensor_reduce(NX[:, h % 2, c, i:i + 1], bank[:, 0:hi - lo], AX_X, ALU.max, negate=True)\
                           .then_inc(s1_read.sem, 1)
                if s1:
                    dve.wait_ge(s1_read.sem, s1_read.at(n, UNITS * (h + 1)))
                    dve.tensor_tensor(NM[:, h % 2, :], NX[:, h % 2, 0, :], NX[:, h % 2, 1, :], ALU.min)\
                       .then_inc(maxima.sem, 1)

            over_groups(dve, step)
            step(NG, 0, False, True, True)
            dve.wait_ge(s_den, 16)
            dve.reciprocal(DEN[:, :], DEN[:, :]).then_inc(s_rden, 1)
            for b in range(NB):
                dve.wait_ge(s_back[b % 2], 32 * (b // 2 + 1))
                dve.tensor_tensor(OA[:, b % 2, :], OA[:, b % 2, :], DA[:, b % 2, :], ALU.mult).then_inc(s_scaled, 1)
                dve.wait_ge(s_out_mm, b + 1)
                x = X[:, b * T:(b + 1) * T]
                for h in range(2):
                    x = X[:, b * T + h * 512:b * T + (h + 1) * 512]
                    last = dve.tensor_tensor(x, s2_ps[b % 2][:, h * 512:(h + 1) * 512], x, ALU.add)
                last.then_inc(s_added, 1)
            dve.wait_ge(s_added, NB)

        @block.gpsimd
        def _(pool):
            pool.memset(VB[:, :, :, :, :], 1.0).then_inc(s_zeros, 1)
            pool.memset(zeros[:, :], 0.0).then_inc(s_zeros, 1)
            pool.wait_ge(norm.s_out, norm.chunks)

            def fetch(b):
                wait(pool, v_mm.sem, v_mm.at(b, 0))
                pool.tensor_copy(XB[:, :], XN[:, bass.ds(b, 1), :].rearrange("p a t -> p (a t)")).then_inc(xb.sem, 1)

            over_sequences(pool, fetch)

            pool.wait_ge(s_zeros, 2)

            def step(n, h, s1, turn, s2):
                i = h % 2
                pool.wait_ge(maxima.sem, maxima.at(n, h + 1))
                wait(pool, s1_mm.sem, s1_mm.at(n, UNITS * (h - 1) + TURN + 1))
                nm, nr = NM[:, i, :], NR[:, i, :]
                part = lambda a: NP[:, i, a, :]
                done = lambda k: pool.wait_ge(parts.sem, parts.at(n, 4 * h + k))
                pool.tensor_tensor(part(0), nm, zeros[:, :], ALU.add).then_inc(parts.sem, 1)
                done(1)
                pool.tensor_tensor(nr, nm, part(0), ALU.subtract).then_inc(parts.sem, 1)
                done(2)
                pool.tensor_tensor(part(1), nr, zeros[:, :], ALU.add).then_inc(parts.sem, 1)
                done(3)
                pool.tensor_tensor(part(2), nr, part(1), ALU.subtract).then_inc(parts.sem, 1)

            over_groups(pool, step)


def output_stage(nc, out, keep):
    X, ident = keep["X"], keep["ident"]
    with nc.cleanup_on_exit(), ExitStack() as ctx:
        sb, ps, sem = allocators(nc, ctx, "out_")
        O = sb("O", [P, NB * NT, P])
        bank = [ps(f"bank{i}", [P, 512]) for i in range(4)]
        s_turned, s_copied, s_stored = sem("turned"), sem("copied"), sem("stored")
        N = NB * NT // 4
        block = ctx.enter_context(nc.Block())

        @block.tensor
        def _(pe):
            for n in range(N):
                if n >= 4:
                    pe.wait_ge(s_copied, n - 3)
                for i in range(4):
                    at = (4 * n + i) * P
                    last = pe.transpose(bank[n % 4][:, i * P:(i + 1) * P], X[:, at:at + P], ident[:, :])
                last.then_inc(s_turned, 1)

        @block.vector
        def _(dve):
            for n in range(N):
                dve.wait_ge(s_turned, n + 1)
                dve.tensor_copy(O[:, 4 * n:4 * n + 4, :].rearrange("p t c -> p (t c)"), bank[n % 4][:, :])\
                   .then_inc(s_copied, 1)

        @block.sync
        def _(sp):
            for n in range(N):
                sp.wait_ge(s_copied, n + 1)
                b, t = n // 2, n % 2 * 4
                sp.dma_start(out[b, t * P:(t + 4) * P, :].rearrange("(t p) c -> p t c", p=P),
                             O[:, 4 * n:4 * n + 4, :]).then_inc(s_stored, 16)
            sp.wait_ge(s_stored, 16 * N)


def network(nc, d, out):
    part = lambda name: {k[len(name) + 1:]: v for k, v in d.items() if k.startswith(name + "_")}
    shared = part("shared")
    with ExitStack() as ctx:
        sb = lambda name, shape, dt=F32: ctx.enter_context(nc.sbuf_tensor(name, shape, dt))
        keep = {"X": sb("X", [P, NB * T]), "ident": sb("ident", [P, P]), "identb": sb("identb", [P, P], BF16),
                "mean": sb("mean", [P, P]), "centre": sb("centre", [P, P]), "eps": sb("eps", [P, 1])}
        attn_a_stage(nc, {**shared, **part("attn_a")}, keep)
        ffn_stage(nc, {**shared, **part("ffn")}, keep, 0)
        attn_b_stage(nc, {**shared, **part("attn_b")}, keep)
        ffn_stage(nc, {**shared, **part("ffn")}, keep, 1)
        output_stage(nc, out, keep)


def causal_masks(np):
    low = np.tril(np.ones((P, P), bool))
    return np.where(np.stack([low, low.T], 1), 0.0, -3e38)


def band_masks(np):
    q = np.arange(P)[:, None]
    k = np.arange(P)[None, :] - WIN + q // WIN * WIN
    m = np.repeat(np.where((k <= q) & (q <= k + WIN), 0.0, -3e38)[:, None, :], NT, 1)
    m[:, 0, :] = np.where(k >= 0, m[:, 0, :], -3e38)
    return m


def xpos_tables(np):
    half = np.arange(0, DH, 2, dtype=np.float32)
    inv_freq = np.float32(1.0) / np.float32(10000.0) ** (half / np.float32(DH))
    t = np.arange(T, dtype=np.float32)
    freqs = (t[:, None] * inv_freq[None, :]).astype(np.float64)
    base = ((half + np.float32(0.4 * DH)) / np.float32(1.4 * DH)).astype(np.float64)
    scale = base[None, :] ** ((t - T // 2) / (WIN // 2)).astype(np.float64)[:, None]
    out = np.zeros((2, T, 2, DH))
    for i, s in enumerate((8.0 * scale, 1.0 / scale)):
        out[0, :, i] = np.concatenate([np.cos(freqs) * s] * 2, 1)
        out[1, :, i] = np.concatenate([-np.sin(freqs) * s, np.sin(freqs) * s], 1)
    return out.reshape(2, NT, P, 2, DH).transpose(0, 2, 1, 3, 4).astype(np.float32)


def rope_tables(np):
    dim = np.arange(0, BD, 2, dtype=np.float32)
    inv_freq = np.float32(1.0) / np.float32(10000.0) ** (dim / np.float32(BD))
    angle = (np.arange(T, dtype=np.float32)[None, :] * inv_freq[:, None]).astype(np.float64)
    angle = np.tile(np.repeat(angle, 2, 0), (BH, 1))
    sign = np.where(np.arange(P) % 2, 1.0, -1.0)[:, None]
    cos, sin = np.cos(angle), np.sin(angle) * sign
    s = 1.0 / np.sqrt(np.float64(BD))
    return np.stack([cos * s, sin * s, cos, sin], 1).astype(np.float32)


def kernel(**inputs):
    import ml_dtypes
    import numpy as np
    import concourse.bacc as bacc
    from concourse.bass_utils import run_bass_kernel_spmd

    a = {name[len("L0_"):]: np.ascontiguousarray(value) for name, value in inputs.items()}
    tiles = lambda v: v.reshape(CT, P).T
    column = lambda v: v.reshape(P, 1)
    pairs = np.arange(P) ^ 1
    bf16 = ml_dtypes.bfloat16
    arrays = {
        "shared_ident": np.eye(P, dtype=np.float32),
        "shared_identb": np.eye(P, dtype=np.float32).astype(bf16),
        "shared_mean": np.full((P, P), 1.0 / P, np.float32),
        "shared_centre": (np.eye(P) - 1.0 / P).astype(np.float32),
        "shared_eps": np.full((P, 1), EPS, np.float32),
        "attn_a_x": a["attn_a_x"],
        "attn_a_pos": np.arange(T, dtype=np.float32).reshape(1, T),
        "attn_a_shift": np.full((P, 1), 10 * math.log(2), np.float32),
        "attn_a_heads16": np.kron(np.eye(P // 16), np.ones((16, 16))).astype(np.float32),
        "attn_a_freqs": tiles(a["attn_a_freqs"]),
        "attn_a_gamma": tiles(np.repeat(a["attn_a_gamma"].reshape(16), 16)),
        "attn_a_conv_w": a["attn_a_conv_w"].reshape(P, 4),
        "attn_a_conv_b": column(a["attn_a_conv_b"]),
        "attn_a_qk_wT": a["attn_a_qk_w"].T,
        "attn_a_v_wT": a["attn_a_v_w"].T,
        "attn_a_g_wT": a["attn_a_g_w"].T,
        "attn_a_o_wT": a["attn_a_o_w"].T,
        "attn_a_g_b": tiles(a["attn_a_g_b"]),
        "attn_a_ln_g": column(a["attn_a_ln_g"]),
        "attn_a_ln_b": column(a["attn_a_ln_b"]),
        "ffn_band": band_masks(np).astype(bf16),
        "ffn_rope": xpos_tables(np),
        "attn_b_causal": causal_masks(np).astype(bf16),
        "attn_b_rope": rope_tables(np),
        "attn_b_WqT": a["attn_b_Wq"].T,
        "attn_b_WqpT": a["attn_b_Wq"][pairs].T,
        "attn_b_WkT": a["attn_b_Wk"].T,
        "attn_b_WkpT": a["attn_b_Wk"][pairs].T,
        "attn_b_WvT": a["attn_b_Wv"].T,
        "attn_b_WoT": a["attn_b_Wo"].T,
    }
    chunked = lambda v: np.concatenate([v, np.zeros(v.shape[:-1] + (NHC * HC - HID_DIM,), v.dtype)], -1)\
        .reshape(v.shape[:-1] + (NHC, HC))
    arrays.update({
        "ffn_wqkv": a["ffn_wqkv"],
        "ffn_wo": a["ffn_wo"],
        "ffn_scales": np.stack([a["ffn_q_scale"], a["ffn_k_scale"]], 1),
        "ffn_columns": np.stack([a["ffn_ln_g"], a["ffn_ln_b"], a["ffn_b2"]], 2),
        "ffn_w1": chunked(a["ffn_w1"].reshape(DEPTH, P, 2, HID_DIM)),
        "ffn_b1": chunked(a["ffn_b1"].reshape(DEPTH, 2, HID_DIM)).transpose(0, 3, 1, 2),
        "ffn_w2": chunked(a["ffn_w2"].transpose(0, 2, 1)).transpose(0, 3, 2, 1),
    })

    nc = bacc.Bacc("TRN2", target_bir_lowering=False, num_devices=1)
    d, feeds = {}, {}
    for name, value in arrays.items():
        feeds[f"in_{name}_dram"] = np.ascontiguousarray(value)
        d[name] = nc.dram_tensor(f"in_{name}_dram", value.shape, mybir.dt.from_np(value.dtype),
                                 kind="ExternalInput").ap()
    out = nc.dram_tensor("out_0_dram", (NB, T, P), F32, kind="ExternalOutput").ap()
    network(nc, d, out)
    return run_bass_kernel_spmd(nc, [feeds], core_ids=[0]).results[0]["out_0_dram"]
```
